# Optimizing a Trainium2 kernel written in Bass

```python
import numpy as np
import jax
import jax.numpy as jnp

def _softmax(x, axis=-1):
    return jax.nn.softmax(x, axis=axis)

def _gelu(x):
    return jax.nn.gelu(x, approximate=True)

def _silu(x):
    return jax.nn.silu(x)

def _sigmoid(x):
    return jax.nn.sigmoid(x)

def _layernorm(x, axis=-1, eps=1e-05):
    m = jnp.mean(x, axis=axis, keepdims=True)
    v = jnp.var(x, axis=axis, keepdims=True)
    return (x - m) / jnp.sqrt(v + eps)

def _scatter_add(tgt, idx, src, axis=0):
    return tgt.at[idx].add(src)

def _segment_sum(src, seg, n):
    return jax.ops.segment_sum(src, seg, n)
kernel_name = 'mk_gnn_resnorm_d1_gnn_r8_78267d'

def setup_inputs(seed: int=0):
    np.random.seed(seed)
    _w = jnp.asarray

    def _rec_inputs():
        import jax
        import jax.numpy as jnp
        _gk = jax.random.key(seed)
        x = -0.0008691 + 1 * jax.random.normal(jax.random.fold_in(_gk, 1), (12500, 128), jnp.float32)
        _s = jax.random.randint(jax.random.fold_in(_gk, 2), (200000,), 0, 12500, jnp.int32)
        _d = jax.random.randint(jax.random.fold_in(_gk, 3), (200000,), 0, 12500, jnp.int32)
        _loop = jnp.arange(12500, dtype=jnp.int32)
        src = jnp.concatenate([_s, _d, _loop])
        dst = jnp.concatenate([_d, _s, _loop])
        _o = jnp.argsort(dst, stable=True)
        src = src[_o]
        dst = dst[_o]
        edge_weight = jax.random.uniform(jax.random.fold_in(_gk, 12), (412500,), jnp.float32, 0.0, 0.999998)
        return (x, src, dst, edge_weight)
    x, src, dst, edge_weight = _rec_inputs()

    def _L0_gnn_setup():
        import jax, jax.numpy as jnp
        import numpy as np
        N = 1250
        E = 80000
        IN_CH = 128
        OUT_CH = 128
        key = jax.random.key(seed)
        k_x, k_ei, k_ea, k_w1, k_b1, k_w2, k_b2 = jax.random.split(key, 7)
        x = jax.random.normal(k_x, (N, IN_CH), dtype=jnp.float32)
        edge_index = jax.random.randint(k_ei, (2, E), 0, N, dtype=jnp.int64)
        edge_attr = jax.random.uniform(k_ea, (E,), dtype=jnp.float32)
        s1 = 1.0 / np.sqrt(2 * IN_CH)
        s2 = 1.0 / np.sqrt(OUT_CH)
        W1 = jax.random.uniform(k_w1, (2 * IN_CH, OUT_CH), jnp.float32, -s1, s1)
        b1 = jax.random.uniform(k_b1, (OUT_CH,), jnp.float32, -s1, s1)
        W2 = jax.random.uniform(k_w2, (OUT_CH, OUT_CH), jnp.float32, -s2, s2)
        b2 = jax.random.uniform(k_b2, (OUT_CH,), jnp.float32, -s2, s2)
        return {'x': x, 'edge_index': edge_index, 'edge_attr': edge_attr, 'W1': W1, 'b1': b1, 'W2': W2, 'b2': b2}
    _L0_gnn_all = _L0_gnn_setup()
    _L0_gnn_in = {k: v for k, v in _L0_gnn_all.items() if k in ('W1', 'b1', 'W2', 'b2')}
    del _L0_gnn_all
    return {'x': x, 'src': src, 'dst': dst, 'edge_weight': edge_weight, 'L0_gnn_W1': _L0_gnn_in['W1'], 'L0_gnn_b1': _L0_gnn_in['b1'], 'L0_gnn_W2': _L0_gnn_in['W2'], 'L0_gnn_b2': _L0_gnn_in['b2']}

def reference(x, src, dst, edge_weight, L0_gnn_W1, L0_gnn_b1, L0_gnn_W2, L0_gnn_b2):
    import jax
    import jax.numpy as jnp

    def _L0_gnn_ref(x, edge_index, edge_attr, W1, b1, W2, b2):
        import jax, jax.numpy as jnp
        import numpy as np
        N = 1250
        E = 80000
        IN_CH = 128
        OUT_CH = 128
        row, col = (edge_index[0], edge_index[1])
        x_i = x[row] * edge_attr[:, None]
        x_j = x[col]
        combined = jnp.concatenate([x_i, x_j], axis=1)
        h = jax.nn.relu(combined @ W1 + b1)
        messages = h @ W2 + b2
        out = jnp.zeros((x.shape[0], messages.shape[1]), dtype=messages.dtype)
        out = out.at[col].add(messages)
        return out
    edge_index = jnp.stack([src, dst])
    x = _layernorm(x + _L0_gnn_ref(x, edge_index, edge_weight, L0_gnn_W1, L0_gnn_b1, L0_gnn_W2, L0_gnn_b2), axis=-1)
    return x

_drawn_inputs = setup_inputs


def setup_inputs(seed=0):
    import zlib

    import numpy as np

    out = dict(_drawn_inputs(seed))
    spreads = {}
    factors = {}
    for name, (base, spread) in spreads.items():
        noise = np.random.default_rng([zlib.crc32(name.encode()), seed]).standard_normal(out[name].shape)
        drawn = base * np.exp(spread * noise) if base else spread * noise
        out[name] = jnp.asarray(drawn.astype(out[name].dtype))
    for name, factor in factors.items():
        out[name] = (out[name] * factor).astype(out[name].dtype)
    return out
```

```python
from contextlib import ExitStack

import concourse.bass as bass
from concourse import mybir

F32 = mybir.dt.float32
I32 = mybir.dt.int32
BF16 = mybir.dt.bfloat16
ALU = mybir.AluOpType
ACT = mybir.ActivationFunctionType
AX = mybir.AxisListType

P = 128
TILES = 8
BLOCK = TILES * P
WINDOW = 64
RING = 4
EPS = 1e-5
DMA = 16


def steps(eng, count, ring, body, ahead=0):
    end = ring + (count - ahead - ring) // ring * ring
    for i in range(ring):
        body(i, i)
    with eng.Fori(ring, end - ring + 1, ring) as i:
        for slot in range(ring):
            body(i + slot, slot)
    for i in range(end, count):
        body(i, i % ring)


def hold(eng, semaphore, value):
    if not isinstance(value, int) or value > 0:
        eng.wait_ge(semaphore, value)


def beyond(i, count):
    return isinstance(i, int) and i >= count


def gnn_kernel(nc, x, src, dst, edge_weight, W1, b1, W2, b2, out):
    N, D = x.shape
    E = src.shape[0]
    assert D == P and W1.shape[0] == 2 * D
    CHUNKS = -(-N // P)
    PAIRS = CHUNKS // 2
    assert CHUNKS % 2 == 0
    LAST = N - (CHUNKS - 1) * P
    NP = CHUNKS * P
    BLOCKS = -(-E // BLOCK)
    GROUPS = -(-BLOCKS // P)
    FULL = E // BLOCK
    REST = E - FULL * BLOCK
    HALF = TILES // 2
    g_last = GROUPS - 1
    TILE_STEPS, INDEX_STEP = 17, 14
    COLS = [(a, g, h) for a in (1, 0, 2) for g in range(GROUPS) for h in range(2)]

    with ExitStack() as ctx:
        def sb(name, shape, dt=F32):
            return ctx.enter_context(nc.sbuf_tensor(name, shape, dt))

        def ps(name, shape, dt=F32):
            return ctx.enter_context(nc.psum_tensor(name, shape, dt))

        def sem(name):
            return ctx.enter_context(nc.semaphore(name))

        A_tab = nc.dram_tensor("A_tab", (NP, D), F32, kind="Internal").ap()
        B_tab = nc.dram_tensor("B_tab", (NP, D), F32, kind="Internal").ap()
        sum_tab = nc.dram_tensor("sum_tab", (NP + P, D + 1), F32, kind="Internal").ap()
        base_tab = nc.dram_tensor("base_tab", (GROUPS * P,), I32, kind="Internal").ap()

        rows = sb("rows", [P, RING, TILES, D])
        ident = sb("ident", [P, P])
        ones = sb("ones", [P, P])
        window_iota = sb("window_iota", [P, WINDOW])
        eps_col = sb("eps_col", [P, 1])
        w1_sb = sb("w1_sb", [P, 2, D])
        w2_sb = sb("w2_sb", [P, D])
        b1_row = sb("b1_row", [1, D])
        b2_row = sb("b2_row", [1, D])
        sumT = sb("sumT", [P, NP])
        raw = sb("raw", [P, max(3 * GROUPS * BLOCK, NP)])
        arrays = raw[:, 0:3 * GROUPS * BLOCK].rearrange("p (a g b) -> p a g b", a=3, g=GROUPS)
        dst_f, src_f, w_f = (arrays[:, a, :, :] for a in range(3))
        dst_i, src_i = dst_f.bitcast(I32), src_f.bitcast(I32)
        degree = raw[0:1, 0:NP]
        src_col = sb("src_col", [P, BLOCKS, TILES], I32)
        meta = sb("meta", [P, BLOCKS, 2, TILES])
        lo = sb("lo", [P, GROUPS])
        hi = sb("hi", [P, GROUPS])
        base_f = sb("base_f", [P, GROUPS])
        base_i = sb("base_i", [P, GROUPS], I32)
        span = sb("span", [P, GROUPS])
        span_p = sb("span_p", [P, 1])
        base_row = sb("base_row", [1, GROUPS * P], I32)
        span_one = sb("span_one", [1, 1])
        span_i = sb("span_i", [1, 1], I32)
        X_RING = 4
        x_in = rows[:, :, 0:2, :]
        xT_sb = sb("xT_sb", [P, 2, 2, P])
        A_sb = sb("A_sb", [P, 2, 2, D])
        B_sb = sb("B_sb", [P, 2, 2, D])
        src_now = sb("src_now", [P, RING, TILES], I32)
        meta_now = sb("meta_now", [P, RING, 2, TILES])
        onehot = sb("onehot", [P, RING, HALF, 2, WINDOW])
        spread = sb("spread", [P, 2, HALF, P], BF16)
        b_part = sb("b_part", [P, 2, 3, D], BF16)
        b_left = sb("b_left", [P, 2, D])
        count = sb("count", [P, 2, 1])
        fold = sb("fold", [P, WINDOW])
        b_win = sb("b_win", [P, 2, D])
        hid = sb("hid", [P, 2, TILES, D])
        OUT_RING = 4
        xe = rows[:, 0, :, :].rearrange("p (s c) d -> p s c d", c=2)
        y = rows[:, 1, :, :].rearrange("p (s c) d -> p s c d", c=2)
        sum_now = sb("sum_now", [P, 2, 2, P])
        degree_now = sb("degree_now", [1, 2, 2, P])
        stats = sb("stats", [P, 2, 2, 6])
        mv = sb("mv", [P, 2, 2, 2])
        std = sb("std", [P, 2, 2])
        rstd = sb("rstd", [P, 2, 2])
        min_tmp = hid[:, 0, :, :].rearrange("p t d -> p (t d)")

        EDGE_COLS = BLOCKS * TILES
        src_cols = src_col[:, :, :].rearrange("p b t -> p (b t)")
        dst_cols = sumT[:, 0:EDGE_COLS]
        w_cols = sumT[:, EDGE_COLS:2 * EDGE_COLS]
        tile_buf = rows[:, :, :, :].rearrange("p r t d -> p (r t d)")
        a_rows, b_rows, equal, earlier, dst_wide, before = (tile_buf[:, i * D:(i + 1) * D] for i in range(6))
        hid_one, sum_old, sum_new, zero_row = (tile_buf[:, 1024 + 256 * i:1024 + 256 * i + D + 1] for i in range(4))
        cols = tile_buf[:, 2048:2056]
        dst_now, w_now, first, is_edge, at_now, trash, n_before, dst_safe = (cols[:, i:i + 1] for i in range(8))
        index_now = sb("index_now", [P, 3], I32)

        spread_ps = ps("spread_ps", [P, 2, HALF, P])
        pre_ps = ps("pre_ps", [P, 2, TILES, D])
        win_ps = ps("win_ps", [P, 2, 512])
        xT_ps = spread_ps
        tab_ps = pre_ps[:, :, 0:HALF, :].rearrange("p s (c h) d -> p s c (h d)", c=2)
        col_ps = win_ps[:, :, :].rearrange("p s (t b) -> p s t b", b=P)

        ld_w = sem("ld_w")
        ld_x = [sem(f"ld_x{i}") for i in range(X_RING)]
        ld_edge = [sem(f"ld_edge{i}") for i in range(3)]
        padded = sem("padded")
        consts = sem("consts")
        xT_ready = sem("xT_ready")
        xT_copied = sem("xT_copied")
        tab_ready = sem("tab_ready")
        tab_copied = sem("tab_copied")
        A_stored = [sem(f"A_stored{i}") for i in range(2)]
        B_stored = [sem(f"B_stored{i}") for i in range(2)]
        prep = sem("prep")
        edge_ready = [sem(f"edge_ready{i}") for i in range(3)]
        base_ready = sem("base_ready")
        base_out = sem("base_out")
        base_in = sem("base_in")
        col_ready = sem("col_ready")
        col_copied = sem("col_copied")
        cleared = sem("cleared")
        span_ready = sem("span_ready")
        span_turned = sem("span_turned")
        flag_ready = sem("flag_ready")
        edges_done = sem("edges_done")
        idx_staged = sem("idx_staged")
        go = sem("go")
        meta_staged = sem("meta_staged")
        landed = [sem(f"landed{i}") for i in range(RING)]
        oh_ready = sem("oh_ready")
        spread_t = sem("spread_t")
        spread_sb = sem("spread_sb")
        win_loaded = [sem(f"win_loaded{i}") for i in range(2)]
        b_split = sem("b_split")
        pre_ready = sem("pre_ready")
        z_ready = sem("z_ready")
        hid_ready = sem("hid_ready")
        sum_ready = sem("sum_ready")
        sum_added = sem("sum_added")
        trash_ready = sem("trash_ready")
        table_zero = sem("table_zero")
        abs_ready = sem("abs_ready")
        abs_turned = sem("abs_turned")
        abs_copied = sem("abs_copied")
        table_clear = sem("table_clear")
        tile_step = sem("tile_step")
        tile_landed = sem("tile_landed")
        dst_turned = sem("dst_turned")
        combined = sem("combined")
        old_landed = sem("old_landed")
        scattered = sem("scattered")
        chunk_loaded = sem("chunk_loaded")
        chunk_turned = sem("chunk_turned")
        chunk_copied = sem("chunk_copied")
        xe_loaded = [sem(f"xe_loaded{i}") for i in range(OUT_RING)]
        sum_staged = sem("sum_staged")
        degree_staged = sem("degree_staged")
        proj_ready = sem("proj_ready")
        y_ready = sem("y_ready")
        st_ready = sem("st_ready")
        mv_ready = sem("mv_ready")
        std_ready = sem("std_ready")
        rstd_ready = sem("rstd_ready")
        o_ready = sem("o_ready")
        o_stored = [sem(f"o_stored{i}") for i in range(OUT_RING)]

        block = ctx.enter_context(nc.Block())

        x_main = x[0:(CHUNKS - 1) * P, :].rearrange("(c p) k -> p c k", p=P)
        out_main = out[0:(CHUNKS - 1) * P, :].rearrange("(c p) k -> p c k", p=P)
        A_rows = A_tab.rearrange("(c p) k -> p c k", p=P)
        B_rows = B_tab.rearrange("(c p) k -> p c k", p=P)
        EDGE_LOADS = DMA * (GROUPS + (1 if REST else 0))

        def load_edges(eng, to, array, signal):
            for g in range(GROUPS):
                n = min(FULL - g * P, P)
                eng.dma_start(to[0:n, g, :], array[g * P * BLOCK:(g * P + n) * BLOCK]
                              .rearrange("(p b) -> p b", b=BLOCK)).then_inc(signal, DMA)
            if REST:
                r = FULL - g_last * P
                eng.dma_start(to[r:r + 1, g_last, 0:REST],
                              array[FULL * BLOCK:E].rearrange("(p b) -> p b", p=1)).then_inc(signal, DMA)

        def rounds(i, slot, ring, each):
            return (i - slot) * (each // ring)

        def fast_or_general(eng, fast, general):
            eng.wait_ge(flag_ready, 1)
            flag = eng.value_load(span_i[0:1, 0:1], min_val=0, max_val=NP)
            with eng.If(flag < WINDOW):
                fast()
            with eng.Else():
                general()

        @block.sync
        def _(sp):
            sp.dma_start(w1_sb[:, :, :], W1.rearrange("(h k) n -> k h n", h=2)).then_inc(ld_w, DMA)
            sp.dma_start(b1_row[:, :], b1.rearrange("(a n) -> a n", a=1)).then_inc(ld_w, DMA)
            sp.dma_start(w2_sb[:, :], W2).then_inc(ld_w, DMA)
            sp.dma_start(b2_row[:, :], b2.rearrange("(a n) -> a n", a=1)).then_inc(ld_w, DMA)
            def load_pair(q, slot):
                hold(sp, xT_ready, q - X_RING + 1)
                if beyond(q, PAIRS - 1):
                    sp.dma_start(x_in[:, slot, 0:1, :], x_main[:, bass.ds(q * 2, 1), :]).then_inc(ld_x[slot], DMA)
                    sp.dma_start(x_in[0:LAST, slot, 1, :], x[(CHUNKS - 1) * P:N, :]).then_inc(ld_x[slot], DMA)
                else:
                    sp.dma_start(x_in[:, slot, :, :], x_main[:, bass.ds(q * 2, 2), :]).then_inc(ld_x[slot], DMA)

            def store_tables(q, slot):
                sp.wait_ge(tab_copied, 2 * q + 2)
                sp.dma_start(A_rows[:, bass.ds(q * 2, 2), :], A_sb[:, slot, :, :]).then_inc(A_stored[slot], DMA)
                sp.dma_start(B_rows[:, bass.ds(q * 2, 2), :], B_sb[:, slot, :, :]).then_inc(B_stored[slot], DMA)
            for q in range(X_RING - 1):
                load_pair(q, q)

            def x_and_tables(q, slot):
                if not beyond(q + X_RING - 1, PAIRS):
                    load_pair(q + X_RING - 1, (slot + X_RING - 1) % X_RING)
                store_tables(q, slot % 2)
            steps(sp, PAIRS, X_RING, x_and_tables, ahead=X_RING)
            sp.wait_ge(B_stored[0], DMA * ((PAIRS + 1) // 2))
            sp.wait_ge(B_stored[1], DMA * (PAIRS // 2))

            sp.wait_ge(base_ready, 1)
            with nc.allow_non_contiguous_dma(reason="512 words, once"):
                sp.dma_start(base_tab.rearrange("(g p) -> p g", p=P), base_i[:, :]).then_inc(base_out, DMA)
            sp.wait_ge(base_out, DMA)
            sp.dma_start(base_row[:, :], base_tab.rearrange("(a n) -> a n", a=1)).then_inc(base_in, DMA)
            sp.wait_ge(base_in, DMA)

            def load_window(s, slot):
                base = sp.value_load(base_row[0:1, bass.ds(s, 1)], min_val=0, max_val=NP - WINDOW)
                hold(sp, b_split, 4 * (s - 1))
                for h in range(2):
                    sp.dma_start(b_win[h * WINDOW:(h + 1) * WINDOW, slot, :],
                                 B_tab[bass.ds(base, WINDOW), :]).then_inc(win_loaded[slot], DMA)

            def zero_and_read_sums():
                sp.wait_ge(table_zero, 1)
                with sp.Fori(0, CHUNKS + 1) as c:
                    sp.dma_start(sum_tab[bass.ds(c * P, P), :], zero_row).then_inc(table_clear, DMA)
                sp.wait_ge(scattered, DMA * EDGE_COLS)
                with sp.Fori(0, CHUNKS) as c:
                    sp.dma_start(sum_old, sum_tab[bass.ds(c * P, P), :]).then_inc(chunk_loaded, DMA)
                    sp.wait_ge(chunk_copied, 2 * c + 2)
                    sp.sem_inc(go, 1)

            fast_or_general(sp, lambda: steps(sp, BLOCKS, 2, load_window), zero_and_read_sums)

            def load_x(q, slot):
                hold(sp, y_ready, q - OUT_RING + 1)
                if beyond(q, PAIRS - 1):
                    sp.dma_start(xe[:, slot, 0:1, :], x_main[:, bass.ds(q * 2, 1), :]).then_inc(xe_loaded[slot], DMA)
                    sp.dma_start(xe[0:LAST, slot, 1, :], x[(CHUNKS - 1) * P:N, :]).then_inc(xe_loaded[slot], DMA)
                else:
                    sp.dma_start(xe[:, slot, :, :], x_main[:, bass.ds(q * 2, 2), :]).then_inc(xe_loaded[slot], DMA)

            def store_out(q, slot):
                sp.wait_ge(o_ready, 2 * q + 2)
                if beyond(q, PAIRS - 1):
                    sp.dma_start(out_main[:, bass.ds(q * 2, 1), :], y[:, slot, 0:1, :]).then_inc(o_stored[slot], DMA)
                    sp.dma_start(out[(CHUNKS - 1) * P:N, :], y[0:LAST, slot, 1, :]).then_inc(o_stored[slot], DMA)
                else:
                    sp.dma_start(out_main[:, bass.ds(q * 2, 2), :], y[:, slot, :, :]).then_inc(o_stored[slot], DMA)

            AHEAD = OUT_RING - 1
            sp.wait_ge(edges_done, 1)
            for q in range(AHEAD):
                load_x(q, q)

            def x_and_out(q, slot):
                if not beyond(q + AHEAD, PAIRS):
                    load_x(q + AHEAD, (slot + AHEAD) % OUT_RING)
                store_out(q, slot)
            steps(sp, PAIRS, OUT_RING, x_and_out, ahead=AHEAD + 1)
            for slot in range(OUT_RING):
                uses = len(range(slot, PAIRS, OUT_RING)) + (1 if slot == (PAIRS - 1) % OUT_RING else 0)
                sp.wait_ge(o_stored[slot], DMA * uses)

        @block.gpsimd
        def _(pool):
            nc.gpsimd.memset(ident[:, :], 0.0).then_inc(consts, 1)
            nc.gpsimd.memset(ones[:, :], 1.0).then_inc(consts, 1)
            pool.wait_ge(consts, 2)
            nc.gpsimd.affine_select(out=ident[:, :], in_=ident[:, :], compare_op=ALU.not_equal, fill=1.0,
                                    base=0, pattern=[[-1, P]], channel_multiplier=1).then_inc(consts, 1)
            nc.gpsimd.iota(window_iota[:, :], pattern=[[1, WINDOW]], base=0, channel_multiplier=0,
                           allow_small_or_imprecise_dtypes=True).then_inc(consts, 1)
            pool.wait_ge(consts, 4)
            for h in range(2):
                half = slice(h * WINDOW, (h + 1) * WINDOW)
                nc.gpsimd.tensor_copy(fold[half, :], ident[half, half]).then_inc(consts, 1)

            pool.wait_ge(A_stored[0], DMA * ((PAIRS + 1) // 2))
            pool.wait_ge(A_stored[1], DMA * (PAIRS // 2))

            def gather(s, slot):
                pool.wait_ge(idx_staged, s + 1)
                hold(pool, z_ready, s - RING + 1)
                pool.sem_inc(go, 1)
                for t in range(TILES):
                    nc.gpsimd.indirect_dma_start(
                        out=rows[:, slot, t, :], out_offset=None, in_=A_tab,
                        in_offset=bass.IndirectOffsetOnAxis(ap=src_now[:, slot, t:t + 1], axis=0),
                    ).then_inc(landed[slot], DMA)

            def general():
                nc.gpsimd.iota(trash, pattern=[[0, 1]], base=NP, channel_multiplier=1,
                               allow_small_or_imprecise_dtypes=True).then_inc(trash_ready, 1)
                nc.gpsimd.affine_select(out=before, in_=ones[:, :], compare_op=ALU.is_gt, fill=0.0, base=0,
                                        pattern=[[-1, P]], channel_multiplier=1).then_inc(trash_ready, 1)
                pool.wait_ge(table_clear, DMA * (CHUNKS + 1))
                for i in range(2):
                    pool.wait_ge(B_stored[i], DMA * ((PAIRS + 1 - i) // 2))
                with pool.Fori(0, EDGE_COLS) as t:
                    pool.wait_ge(tile_step, TILE_STEPS * t + 4)
                    pool.sem_inc(go, 1)
                    for to, table, k in ((a_rows, A_tab, 0), (b_rows, B_tab, 1)):
                        nc.gpsimd.indirect_dma_start(
                            out=to, out_offset=None, in_=table,
                            in_offset=bass.IndirectOffsetOnAxis(ap=index_now[:, k:k + 1], axis=0),
                        ).then_inc(tile_landed, DMA)
                    pool.wait_ge(tile_step, TILE_STEPS * t + INDEX_STEP)
                    pool.sem_inc(go, 1)
                    nc.gpsimd.indirect_dma_start(
                        out=sum_old, out_offset=None, in_=sum_tab,
                        in_offset=bass.IndirectOffsetOnAxis(ap=index_now[:, 2:3], axis=0),
                    ).then_inc(old_landed, DMA)
                    pool.wait_ge(tile_step, TILE_STEPS * t + TILE_STEPS)
                    pool.sem_inc(go, 1)
                    nc.gpsimd.indirect_dma_start(
                        out=sum_tab, out_offset=bass.IndirectOffsetOnAxis(ap=index_now[:, 2:3], axis=0),
                        in_=sum_new, in_offset=None).then_inc(scattered, DMA)

            fast_or_general(pool, lambda: steps(pool, BLOCKS, RING, gather), general)

            pool.wait_ge(edges_done, 1)

            def stage_degree(q, slot):
                hold(pool, proj_ready, q - 1)
                nc.gpsimd.tensor_copy(degree_now[0:1, slot, :, :], degree[0:1, bass.ds(q * 2 * P, 2 * P)]
                                      .rearrange("p (c n) -> p c n", c=2)).then_inc(degree_staged, 1)
            steps(pool, PAIRS, 2, stage_degree)

        @block.scalar
        def _(act):
            act.wait_ge(padded, 3)
            load_edges(act, dst_i, dst, ld_edge[0])
            load_edges(act, src_i, src, ld_edge[1])
            load_edges(act, w_f, edge_weight, ld_edge[2])

            def copy_xT(q, slot):
                act.wait_ge(xT_ready, q + 1)
                hold(act, tab_ready, q - 1)
                nc.scalar.copy(xT_sb[:, slot, :, :], xT_ps[:, slot, 0:2, :]).then_inc(xT_copied, 1)

            def copy_tables(q, slot):
                act.wait_ge(tab_ready, q + 1)
                hold(act, A_stored[slot], rounds(q, slot, 2, DMA))
                hold(act, B_stored[slot], rounds(q, slot, 2, DMA))
                nc.scalar.copy(A_sb[:, slot, :, :], tab_ps[:, slot, :, 0:D]).then_inc(tab_copied, 1)
                nc.scalar.copy(B_sb[:, slot, :, :], tab_ps[:, slot, :, D:2 * D]).then_inc(tab_copied, 1)

            copy_xT(0, 0)

            def tables(q, slot):
                if not beyond(q + 1, PAIRS):
                    copy_xT(q + 1, 1 - slot)
                copy_tables(q, slot)
            steps(act, PAIRS, 2, tables, ahead=1)

            def copy_spread(s, slot):
                act.wait_ge(spread_t, s + 1)
                hold(act, pre_ready, s - 1)
                hold(act, sum_ready, s - 1)
                nc.scalar.activation(spread[:, slot, :, :], spread_ps[:, slot, :, :], ACT.Copy,
                                     accum_out=count[:, slot, :]).then_inc(spread_sb, 1)


            def hidden(s, slot):
                act.wait_ge(z_ready, s + 1)
                nc.scalar.activation(hid[:, slot, :, :], hid[:, slot, :, :], ACT.Relu).then_inc(hid_ready, 1)
                if not beyond(s + 2, BLOCKS):
                    copy_spread(s + 2, slot)

            def fast():
                copy_spread(0, 0)
                copy_spread(1, 1)
                steps(act, BLOCKS, 2, hidden, ahead=2)

            fast_or_general(act, fast, lambda: act.wait_ge(edges_done, 1))

            act.wait_ge(edges_done, 1)

            def stage_sum(q, slot):
                hold(act, proj_ready, q - 1)
                nc.scalar.copy(sum_now[:, slot, :, :], sumT[:, bass.ds(q * 2 * P, 2 * P)]
                               .rearrange("p (c n) -> p c n", c=2)).then_inc(sum_staged, 1)

            def stdev(q, slot):
                act.wait_ge(mv_ready, 2 * q + 2)
                hold(act, rstd_ready, q - 1)
                nc.scalar.activation(std[:, slot, :], mv[:, slot, :, 1], ACT.Sqrt, bias=eps_col[:, 0:1],
                                     scale=1.0).then_inc(std_ready, 1)
            stage_sum(0, 0)

            def stage_and_stdev(q, slot):
                if not beyond(q + 1, PAIRS):
                    stage_sum(q + 1, 1 - slot)
                stdev(q, slot)
            steps(act, PAIRS, 2, stage_and_stdev, ahead=1)

        @block.vector
        def _(dve):
            nc.vector.memset(dst_i[:, g_last, :], -1).then_inc(padded, 1)
            nc.vector.memset(src_f[:, g_last, :], 0.0).then_inc(padded, 1)
            nc.vector.memset(w_f[:, g_last, :], 0.0).then_inc(padded, 1)
            nc.vector.memset(eps_col[:, :], EPS).then_inc(padded, 1)

            done = [0]

            def step(instruction):
                done[0] += 1
                instruction.then_inc(prep, 1)
                dve.wait_ge(prep, done[0])

            dve.wait_ge(ld_edge[1], EDGE_LOADS)
            for g in range(GROUPS):
                nc.vector.tensor_copy(src_f[:, g, :], src_i[:, g, :]).then_inc(edge_ready[1], 1)
            dve.wait_ge(ld_edge[0], EDGE_LOADS)
            for g in range(GROUPS):
                step(nc.vector.tensor_copy(dst_f[:, g, :], dst_i[:, g, :]))
                if g == g_last:
                    step(nc.vector.tensor_scalar(min_tmp, dst_f[:, g, :], 0.0, float(2 * NP),
                                                 ALU.is_lt, ALU.mult))
                    step(nc.vector.tensor_tensor(min_tmp, min_tmp, dst_f[:, g, :], ALU.add))
                    step(nc.vector.tensor_reduce(lo[:, g:g + 1], min_tmp, AX.X, ALU.min))
                else:
                    step(nc.vector.tensor_reduce(lo[:, g:g + 1], dst_f[:, g, :], AX.X, ALU.min))
                step(nc.vector.tensor_reduce(hi[:, g:g + 1], dst_f[:, g, :], AX.X, ALU.max))
            step(nc.vector.tensor_scalar(base_f[:, :], lo[:, :], float(NP - WINDOW), None, ALU.min))
            nc.vector.tensor_copy(base_i[:, :], base_f[:, :]).then_inc(base_ready, 1)
            step(nc.vector.tensor_tensor(span[:, :], hi[:, :], base_f[:, :], ALU.subtract))
            nc.vector.tensor_reduce(span_p[:, :], span[:, :], AX.X, ALU.max).then_inc(span_ready, 1)
            for g in range(GROUPS):
                nc.vector.tensor_scalar(dst_f[:, g, :], dst_f[:, g, :], base_f[:, g:g + 1], None,
                                        ALU.subtract).then_inc(edge_ready[0], 1)

            dve.wait_ge(span_turned, 1)
            step(nc.vector.tensor_reduce(span_one[:, :], win_ps[0:1, 0, 0:P], AX.X, ALU.max))
            nc.vector.tensor_copy(span_i[:, :], span_one[:, :]).then_inc(flag_ready, 1)

            for j, (a, g, h) in enumerate(COLS):
                n = min(BLOCKS - g * P, P)
                dve.wait_ge(col_ready, j + 1)
                to = src_col if a == 1 else meta[:, :, 0 if a == 0 else 1, :]
                nc.vector.tensor_copy(to[:, g * P:g * P + n, h * HALF:(h + 1) * HALF],
                                      col_ps[:, j % 2, :, 0:n].rearrange("p t b -> p b t")).then_inc(col_copied, 1)

            def stage_index(s, slot):
                nc.vector.tensor_copy(src_now[:, slot, :], src_col[:, bass.ds(s, 1), :]
                                      .rearrange("p a t -> p (a t)")).then_inc(idx_staged, 1)

            def stage_meta(s, slot):
                hold(dve, z_ready, s - RING + 1)
                nc.vector.tensor_copy(meta_now[:, slot, :, :], meta[:, bass.ds(s, 1), :, :]
                                      .rearrange("p a m t -> p (a m) t")).then_inc(meta_staged, 1)

            def one_hots(s, slot):
                dve.wait_ge(meta_staged, s + 1)
                hold(dve, sum_ready, s - RING + 1)
                for t in range(TILES):
                    last = nc.vector.tensor_scalar(onehot[:, slot, t % HALF, t // HALF, :], window_iota[:, :],
                                                   meta_now[:, slot, 0, t:t + 1], None, ALU.is_equal)
                last.then_inc(oh_ready, 1)

            def pre_hidden(s, slot):
                dve.wait_ge(pre_ready, s + 1)
                dve.wait_ge(landed[slot], rounds(s, slot, RING, DMA * TILES) + DMA * TILES)
                hold(dve, sum_ready, s - 1)
                for t in range(TILES):
                    last = nc.vector.scalar_tensor_tensor(
                        out=hid[:, slot % 2, t, :], in0=rows[:, slot, t, :], scalar=meta_now[:, slot, 1, t:t + 1],
                        in1=pre_ps[:, slot % 2, t, :], op0=ALU.mult, op1=ALU.add)
                last.then_inc(z_ready, 1)

            def add_sums(s, slot):
                base = dve.value_load(base_row[0:1, bass.ds(s, 1)], min_val=0, max_val=NP - WINDOW)
                dve.wait_ge(sum_ready, s + 1)
                hold(dve, sum_added, 2 * s)
                to = sumT[:, bass.ds(base, WINDOW)]
                nc.vector.tensor_tensor(to, to, win_ps[:, slot, 0:WINDOW], ALU.add).then_inc(sum_added, 1)
                to = degree[0:1, bass.ds(base, WINDOW)]
                nc.vector.tensor_tensor(to, to, win_ps[0:1, slot, WINDOW:2 * WINDOW], ALU.add).then_inc(sum_added, 1)

            def split_window(s, slot, part):
                if part == 0:
                    dve.wait_ge(win_loaded[slot], rounds(s, slot, 2, 2 * DMA) + 2 * DMA)
                    hold(dve, pre_ready, s - 1)
                else:
                    dve.wait_ge(b_split, 4 * s + part)
                if part % 2 == 0:
                    left = b_win if part == 0 else b_left
                    nc.vector.tensor_copy(b_part[:, slot, part // 2, :], left[:, slot, :]).then_inc(b_split, 1)
                else:
                    left, to = (b_win[:, slot, :], b_left[:, slot, :]) if part == 1 else \
                        (b_left[:, slot, :], b_part[:, slot, 2, :])
                    nc.vector.tensor_tensor(to, left, b_part[:, slot, part // 2, :],
                                            ALU.subtract).then_inc(b_split, 1)

            dve.wait_ge(col_copied, len(COLS))
            def edges(s, slot):
                if not beyond(s + RING - 1, BLOCKS):
                    stage_index(s + RING - 1, (slot + RING - 1) % RING)
                ahead = not beyond(s + 2, BLOCKS)
                if ahead:
                    stage_meta(s + 2, (slot + 2) % RING)
                    split_window(s + 2, slot % 2, 0)
                    one_hots(s + 2, (slot + 2) % RING)
                    split_window(s + 2, slot % 2, 1)
                pre_hidden(s, slot)
                if ahead:
                    split_window(s + 2, slot % 2, 2)
                if not beyond(-s, 0):
                    add_sums(s - 1, (slot - 1) % 2)
                if ahead:
                    split_window(s + 2, slot % 2, 3)
            def fast():
                for s in range(RING - 1):
                    stage_index(s, s)
                for s in range(2):
                    stage_meta(s, s)
                    one_hots(s, s)
                nc.vector.memset(sumT[:, :], 0.0).then_inc(cleared, 1)
                dve.wait_ge(col_ready, len(COLS))
                nc.vector.memset(degree, 0.0).then_inc(cleared, 1)
                dve.wait_ge(cleared, 2)
                dve.wait_ge(base_in, DMA)
                for s in range(2):
                    for part in range(4):
                        split_window(s, s, part)
                steps(dve, BLOCKS, RING, edges, ahead=RING - 1)
                add_sums(BLOCKS - 1, (BLOCKS - 1) % 2)
                dve.wait_ge(sum_added, 2 * BLOCKS)
                dve.sem_inc(edges_done, 1)

            def general():
                nc.vector.memset(zero_row, 0.0).then_inc(table_zero, 1)
                nc.vector.memset(hid_one[:, D:D + 1], 1.0).then_inc(abs_copied, 1)
                for g in range(GROUPS):
                    nc.vector.tensor_scalar(dst_f[:, g, :], dst_f[:, g, :], base_f[:, g:g + 1], None,
                                            ALU.add).then_inc(abs_ready, 1)
                nc.vector.tensor_copy(w_cols.rearrange("p (b t) -> p b t", t=TILES),
                                      meta[:, :, 1, :]).then_inc(abs_copied, 1)
                for j in range(2 * GROUPS):
                    g, h = j // 2, j % 2
                    n = min(BLOCKS - g * P, P)
                    dve.wait_ge(abs_turned, j + 1)
                    nc.vector.tensor_copy(dst_cols.rearrange("p (b t) -> p b t", t=TILES)
                                          [:, g * P:g * P + n, h * HALF:(h + 1) * HALF],
                                          col_ps[:, j % 2, :, 0:n].rearrange("p t b -> p b t")).then_inc(abs_copied, 1)
                dve.wait_ge(abs_copied, 2 * GROUPS + 2)
                dve.wait_ge(trash_ready, 2)

                with dve.Fori(0, EDGE_COLS) as t:
                    taken = [0]

                    def then(instruction):
                        taken[0] += 1
                        instruction.then_inc(tile_step, 1)
                        dve.wait_ge(tile_step, TILE_STEPS * t + taken[0])

                    then(nc.vector.tensor_copy(dst_now, dst_cols[:, bass.ds(t, 1)]))
                    then(nc.vector.tensor_copy(w_now, w_cols[:, bass.ds(t, 1)]))
                    then(nc.vector.tensor_copy(index_now[:, 0:1], src_cols[:, bass.ds(t, 1)]))
                    then(nc.vector.tensor_scalar(index_now[:, 1:2], dst_now, 0.0, None, ALU.max))
                    then(nc.vector.tensor_scalar(dst_wide, ones[:, :], dst_now, None, ALU.mult))
                    dve.wait_ge(dst_turned, t + 1)
                    then(nc.vector.tensor_scalar(equal, spread_ps[:, 0, 0, :], dst_now, None, ALU.is_equal))
                    then(nc.vector.tensor_tensor(earlier, equal, before, ALU.mult))
                    then(nc.vector.tensor_reduce(n_before, earlier, AX.X, ALU.add))
                    then(nc.vector.tensor_scalar(first, n_before, 0.5, None, ALU.is_lt))
                    then(nc.vector.tensor_scalar(is_edge, dst_now, 0.0, None, ALU.is_ge))
                    then(nc.vector.tensor_tensor(first, first, is_edge, ALU.mult))
                    then(nc.vector.tensor_tensor(at_now, dst_now, trash, ALU.subtract))
                    then(nc.vector.tensor_tensor(at_now, at_now, first, ALU.mult))
                    then(nc.vector.tensor_tensor(index_now[:, 2:3], at_now, trash, ALU.add))
                    assert taken[0] == INDEX_STEP
                    dve.wait_ge(tile_landed, 2 * DMA * t + 2 * DMA)
                    then(nc.vector.scalar_tensor_tensor(out=hid_one[:, 0:D], in0=a_rows, scalar=w_now, in1=b_rows,
                                                        op0=ALU.mult, op1=ALU.add))
                    then(nc.vector.tensor_scalar(hid_one[:, 0:D], hid_one[:, 0:D], 0.0, None, ALU.max))
                    assert taken[0] == INDEX_STEP + 2
                    dve.wait_ge(combined, t + 1)
                    dve.wait_ge(old_landed, DMA * t + DMA)
                    then(nc.vector.tensor_tensor(sum_new, sum_old, win_ps[:, 0, 0:D + 1], ALU.add))
                    assert taken[0] == TILE_STEPS
                    dve.wait_ge(scattered, DMA * t + DMA)

                with dve.Fori(0, CHUNKS) as c:
                    dve.wait_ge(chunk_turned, c + 1)
                    nc.vector.tensor_copy(sumT[:, bass.ds(c * P, P)], spread_ps[:, 0, 0, :]).then_inc(chunk_copied, 1)
                    nc.vector.tensor_copy(degree[0:1, bass.ds(c * P, P)],
                                          spread_ps[0:1, 0, 1, :]).then_inc(chunk_copied, 1)
                dve.wait_ge(chunk_copied, 2 * CHUNKS)
                dve.sem_inc(edges_done, 1)

            fast_or_general(dve, fast, general)

            def add_x(q, slot):
                dve.wait_ge(proj_ready, q + 1)
                extra = DMA if beyond(q, PAIRS - 1) else 0
                dve.wait_ge(xe_loaded[slot], rounds(q, slot, OUT_RING, DMA) + DMA + extra)
                hold(dve, o_stored[slot], rounds(q, slot, OUT_RING, DMA))
                nc.vector.tensor_tensor(y[:, slot, :, :], xe[:, slot, :, :],
                                        win_ps[:, slot % 2, 0:2 * D].rearrange("p (c d) -> p c d", c=2),
                                        ALU.add).then_inc(y_ready, 1)

            def scale(q, slot):
                dve.wait_ge(rstd_ready, q + 1)
                for c in range(2):
                    nc.vector.tensor_scalar(y[:, slot, c, :], y[:, slot, c, :], mv[:, slot % 2, c, 0:1],
                                            rstd[:, slot % 2, c:c + 1], ALU.subtract, ALU.mult).then_inc(o_ready, 1)

            def norm(q, slot):
                add_x(q, slot)
                if not beyond(-q, 0):
                    dve.wait_ge(std_ready, q)
                    nc.vector.reciprocal(rstd[:, (slot - 1) % 2, :], std[:, (slot - 1) % 2, :]).then_inc(rstd_ready, 1)
                dve.wait_ge(y_ready, q + 1)
                for c in range(2):
                    nc.vector.bn_stats(stats[:, slot % 2, c, :], y[:, slot, c, :]).then_inc(st_ready, 1)
                if not beyond(-q, 0):
                    scale(q - 1, (slot - 1) % OUT_RING)
                dve.wait_ge(st_ready, 2 * q + 2)
                dve.sem_inc(go, 1)
                for c in range(2):
                    nc.vector.bn_aggr(mv[:, slot % 2, c, :], stats[:, slot % 2, c, :]).then_inc(mv_ready, 1)
            steps(dve, PAIRS, OUT_RING, norm)
            dve.wait_ge(std_ready, PAIRS)
            nc.vector.reciprocal(rstd[:, (PAIRS - 1) % 2, :], std[:, (PAIRS - 1) % 2, :]).then_inc(rstd_ready, 1)
            scale(PAIRS - 1, (PAIRS - 1) % OUT_RING)

        @block.tensor
        def _(pe):
            pe.wait_ge(consts, 6)
            pe.wait_ge(ld_w, 4 * DMA)

            def transpose_x(q, slot):
                extra = DMA if beyond(q, PAIRS - 1) else 0
                pe.wait_ge(ld_x[slot], rounds(q, slot, X_RING, DMA) + DMA + extra)
                hold(pe, xT_copied, q - 1)
                for c in range(2):
                    last = nc.tensor.transpose(xT_ps[:, slot % 2, c, :], x_in[:, slot, c, :], ident[:, :])
                last.then_inc(xT_ready, 1)

            def products(q, slot):
                pe.wait_ge(xT_copied, q + 1)
                hold(pe, tab_copied, 2 * (q - 1))
                for c in range(2):
                    nc.tensor.matmul(tab_ps[:, slot, c, :], xT_sb[:, slot, c, :],
                                     w1_sb[:, :, :].rearrange("p h n -> p (h n)"), start=True, stop=False)
                    last = nc.tensor.matmul(tab_ps[:, slot, c, D:2 * D], ones[0:1, :], b1_row[:, :],
                                            start=False, stop=True)
                last.then_inc(tab_ready, 1)

            transpose_x(0, 0)

            def tables(q, slot):
                if not beyond(q + 1, PAIRS):
                    transpose_x(q + 1, (slot + 1) % X_RING)
                products(q, slot % 2)
            steps(pe, PAIRS, X_RING, tables, ahead=2)

            pe.wait_ge(span_ready, 1)
            nc.tensor.transpose(win_ps[0:1, 0, 0:P], span_p[:, :], ident[:, :]).then_inc(span_turned, 1)
            pe.wait_ge(flag_ready, 1)

            for j, (a, g, h) in enumerate(COLS):
                n = min(BLOCKS - g * P, P)
                pe.wait_ge(edge_ready[a] if a < 2 else ld_edge[2], g + 1 if a < 2 else EDGE_LOADS)
                hold(pe, col_copied, j - 1)
                for t in range(HALF):
                    at = (h * HALF + t) * P
                    last = nc.tensor.transpose(col_ps[:, j % 2, t, 0:n], arrays[0:n, a, g, at:at + P],
                                               ident[0:n, 0:n])
                last.then_inc(col_ready, 1)

            def spread_one_hots(s, slot):
                pe.wait_ge(oh_ready, s + 1)
                hold(pe, spread_sb, s - 1)
                for t in range(HALF):
                    last = nc.tensor.transpose(spread_ps[:, slot % 2, t, :], onehot[:, slot, t, :, :]
                                               .rearrange("p h w -> p (h w)"), ident[:, :])
                last.then_inc(spread_t, 1)

            def spread_window(s, slot):
                pe.wait_ge(spread_sb, s + 1)
                pe.wait_ge(b_split, 4 * s + 4)
                hold(pe, z_ready, s - 1)
                for t in range(TILES):
                    h = t // HALF
                    half = slice(h * WINDOW, (h + 1) * WINDOW)
                    for part in range(3):
                        last = nc.tensor.matmul(pre_ps[:, slot, t, :], spread[half, slot, t % HALF, :],
                                                b_part[half, slot, part, :], start=(part == 0), stop=(part == 2))
                last.then_inc(pre_ready, 1)

            def sum_edges(s, slot):
                pe.wait_ge(hid_ready, s + 1)
                hold(pe, sum_added, 2 * (s - 1))
                ring_slot, slot = slot, slot % 2
                for t in range(TILES):
                    nc.tensor.matmul(win_ps[:, slot, 0:WINDOW], hid[:, slot, t, :],
                                     onehot[:, ring_slot, t % HALF, t // HALF, :],
                                     start=(t == 0), stop=(t == TILES - 1))
                nc.tensor.matmul(win_ps[0:1, slot, WINDOW:2 * WINDOW], count[:, slot, :], fold[:, :],
                                 start=True, stop=True).then_inc(sum_ready, 1)

            def edges(s, slot):
                if not beyond(s + 2, BLOCKS):
                    spread_one_hots(s + 2, (slot + 2) % RING)
                if not beyond(s + 1, BLOCKS):
                    spread_window(s + 1, (slot + 1) % 2)
                sum_edges(s, slot)

            def fast():
                spread_one_hots(0, 0)
                spread_one_hots(1, 1)
                spread_window(0, 0)
                steps(pe, BLOCKS, RING, edges, ahead=2)

            def general():
                for j in range(2 * GROUPS):
                    g, h = j // 2, j % 2
                    n = min(BLOCKS - g * P, P)
                    pe.wait_ge(abs_ready, g + 1)
                    hold(pe, abs_copied, j + 1)
                    for t in range(HALF):
                        at = (h * HALF + t) * P
                        last = nc.tensor.transpose(col_ps[:, j % 2, t, 0:n], dst_f[0:n, g, at:at + P],
                                                   ident[0:n, 0:n])
                    last.then_inc(abs_turned, 1)
                with pe.Fori(0, EDGE_COLS) as t:
                    pe.wait_ge(tile_step, TILE_STEPS * t + 5)
                    nc.tensor.transpose(spread_ps[:, 0, 0, :], dst_wide, ident[:, :]).then_inc(dst_turned, 1)
                    pe.wait_ge(tile_step, TILE_STEPS * t + INDEX_STEP + 2)
                    nc.tensor.matmul(win_ps[:, 0, 0:D + 1], equal, hid_one, start=True,
                                     stop=True).then_inc(combined, 1)
                with pe.Fori(0, CHUNKS) as c:
                    pe.wait_ge(chunk_loaded, DMA * c + DMA)
                    nc.tensor.transpose(spread_ps[:, 0, 0, :], sum_old[:, 0:D], ident[:, :])
                    nc.tensor.transpose(spread_ps[0:1, 0, 1, :], sum_old[:, D:D + 1],
                                        ident[:, :]).then_inc(chunk_turned, 1)

            fast_or_general(pe, fast, general)

            def project(q, slot):
                pe.wait_ge(sum_staged, q + 1)
                pe.wait_ge(degree_staged, q + 1)
                hold(pe, y_ready, q - 1)
                for c in range(2):
                    nc.tensor.matmul(win_ps[:, slot, c * D:(c + 1) * D], sum_now[:, slot, c, :], w2_sb[:, :],
                                     start=True, stop=False)
                    last = nc.tensor.matmul(win_ps[:, slot, c * D:(c + 1) * D], degree_now[0:1, slot, c, :], b2_row[:, :],
                                            start=False, stop=True)
                last.then_inc(proj_ready, 1)
            steps(pe, PAIRS, 2, project)


_INS = ['x', 'src', 'dst', 'edge_weight', 'L0_gnn_W1', 'L0_gnn_b1', 'L0_gnn_W2', 'L0_gnn_b2']


def kernel(**inputs):
    import numpy as _np
    import concourse.bacc as _bacc
    from concourse import mybir as _mybir
    from concourse.bass_utils import run_bass_kernel_spmd as _run

    nc = _bacc.Bacc("TRN2", target_bir_lowering=False, num_devices=1)
    arrays, args = {}, []
    for name in _INS:
        a = _np.ascontiguousarray(inputs[name])
        arrays[f"in_{name}_dram"] = a
        args.append(nc.dram_tensor(f"in_{name}_dram", a.shape, _mybir.dt.from_np(a.dtype), kind="ExternalInput").ap())
    args.append(nc.dram_tensor("out_0_dram", arrays["in_x_dram"].shape, F32, kind="ExternalOutput").ap())
    gnn_kernel(nc, *args)
    r = _run(nc, [arrays], core_ids=[0])
    return r.results[0]["out_0_dram"]
```

```python
from contextlib import ExitStack

import concourse.bass as bass
from concourse import mybir

F32 = mybir.dt.float32
I32 = mybir.dt.int32
BF16 = mybir.dt.bfloat16
ALU = mybir.AluOpType
ACT = mybir.ActivationFunctionType
AX = mybir.AxisListType

P = 128
TILES = 8
BLOCK = TILES * P
WINDOW = 64
RING = 4
EPS = 1e-5
DMA = 16


def steps(eng, count, ring, body, ahead=0, first=0):
    start = max(first, ring)
    end = start + (count - ahead - start) // ring * ring
    assert end > start
    for i in range(first, start):
        body(i, i)
    with eng.Fori(start, end - ring + 1, ring) as i:
        for slot in range(ring):
            body(i + slot, slot)
    for i in range(end, count):
        body(i, i % ring)


def hold(eng, semaphore, value):
    if not isinstance(value, int) or value > 0:
        eng.wait_ge(semaphore, value)


def beyond(i, count):
    return isinstance(i, int) and i >= count


def gnn_kernel(nc, x, src, dst, edge_weight, W1, b1, W2, b2, out):
    N, D = x.shape
    E = src.shape[0]
    assert D == P and W1.shape[0] == 2 * D
    CHUNKS = -(-N // P)
    QUADS = -(-CHUNKS // 4)
    SPLIT = QUADS // 8 * 4
    LAST = N - (CHUNKS - 1) * P
    NP = CHUNKS * P
    BLOCKS = -(-E // BLOCK)
    GROUPS = -(-BLOCKS // P)
    FULL = E // BLOCK
    REST = E - FULL * BLOCK
    HALF = TILES // 2
    g_last = GROUPS - 1
    TILE_STEPS, INDEX_STEP = 17, 14
    COLS = [(a, g, h) for a in (1, 0, 2) for g in range(GROUPS) for h in range(2)]
    SRC_COLS, OTHER_COLS = range(2 * GROUPS), range(2 * GROUPS, 6 * GROUPS)

    with ExitStack() as ctx:
        def sb(name, shape, dt=F32):
            return ctx.enter_context(nc.sbuf_tensor(name, shape, dt))

        def ps(name, shape, dt=F32):
            return ctx.enter_context(nc.psum_tensor(name, shape, dt))

        def sem(name):
            return ctx.enter_context(nc.semaphore(name))

        A_tab = nc.dram_tensor("A_tab", (NP, D), F32, kind="Internal").ap()
        B_tab = nc.dram_tensor("B_tab", (NP, D), F32, kind="Internal").ap()
        sum_tab = nc.dram_tensor("sum_tab", (NP + P, D + 1), F32, kind="Internal").ap()
        base_tab = nc.dram_tensor("base_tab", (GROUPS * P,), I32, kind="Internal").ap()

        rows = sb("rows", [P, RING, TILES, D])
        ident = sb("ident", [P, P])
        ones = sb("ones", [P, P])
        window_iota = sb("window_iota", [P, WINDOW])
        eps_col = sb("eps_col", [P, 1])
        zeros = sb("zeros", [P, 4 * P])
        w1_sb = sb("w1_sb", [P, 2, D])
        w2_sb = sb("w2_sb", [P, D])
        bias_rows = sb("bias_rows", [1, 2, D])
        bias_wide = sb("bias_wide", [P, 2, D])
        sumT = sb("sumT", [P, NP])
        arrays = sb("arrays", [P, 3, GROUPS, BLOCK])
        dst_f, src_f, w_f = (arrays[:, a, :, :] for a in range(3))
        dst_i, src_i = dst_f.bitcast(I32), src_f.bitcast(I32)
        src_col = sb("src_col", [P, BLOCKS, TILES], I32)
        meta = sb("meta", [P, BLOCKS, 2, TILES])
        lo = sb("lo", [P, GROUPS])
        hi = sb("hi", [P, GROUPS])
        base_f = sb("base_f", [P, GROUPS])
        base_i = sb("base_i", [P, GROUPS], I32)
        span = sb("span", [P, GROUPS])
        span_p = sb("span_p", [P, 1])
        base_row = sb("base_row", [1, GROUPS * P], I32)
        span_one = sb("span_one", [1, 1])
        span_i = sb("span_i", [1, 1], I32)
        NODE_RING = 4
        x_in = rows[:, :, 0:4, :]
        A_sb = rows[:, :, 4:8, :]
        xT_sb = sb("xT_sb", [P, 2, 4, P])
        src_now = sb("src_now", [P, RING, TILES], I32)
        meta_now = sb("meta_now", [P, RING, 2, TILES])
        onehot = sb("onehot", [P, RING, HALF, 2, WINDOW])
        spread = sb("spread", [P, 2, HALF, P], BF16)
        b_part = sb("b_part", [P, 2, 3, D], BF16)
        b_left = sb("b_left", [P, 2, D])
        count = sb("count", [P, RING, 1])
        fold = sb("fold", [P, WINDOW])
        b_win = sb("b_win", [P, 2, D])
        fold_count = sb("fold_count", [P, 2, WINDOW])
        win_sum = sb("win_sum", [P, 2, WINDOW])
        hid = sb("hid", [P, 2, TILES, D])
        B_sb = hid[:, :, :, :].rearrange("p s (h c) d -> p (s h) c d", c=4)
        xe = rows[:, :, 0:4, :]
        y = rows[:, :, 4:8, :]
        sum_now = xT_sb
        stats = sb("stats", [P, 2, 4, 6])
        mv = sb("mv", [P, 2, 4, 2])
        std = sb("std", [P, 2, 4])
        rstd = sb("rstd", [P, 2, 4])
        shift = sb("shift", [P, 2, 4])
        min_tmp = hid[:, 0, :, :].rearrange("p t d -> p (t d)")

        EDGE_COLS = BLOCKS * TILES
        src_cols = src_col[:, :, :].rearrange("p b t -> p (b t)")
        dst_cols = sumT[:, 0:EDGE_COLS]
        w_cols = sumT[:, EDGE_COLS:2 * EDGE_COLS]
        tile_buf = rows[:, :, :, :].rearrange("p r t d -> p (r t d)")
        a_rows, b_rows, equal, earlier, dst_wide, before = (tile_buf[:, i * D:(i + 1) * D] for i in range(6))
        hid_one, sum_old, sum_new, zero_row = (tile_buf[:, 1024 + 256 * i:1024 + 256 * i + D + 1] for i in range(4))
        cols = tile_buf[:, 2048:2056]
        dst_now, w_now, first, is_edge, at_now, trash, n_before, dst_safe = (cols[:, i:i + 1] for i in range(8))
        hid_T = tile_buf[:, 2176:2304]
        degree_T = tile_buf[0:1, 2304:2432]
        index_now = sb("index_now", [P, 3], I32)

        spread_ps = ps("spread_ps", [P, 2, HALF, P])
        pre_ps = ps("pre_ps", [P, 2, TILES, D])
        win_ps = ps("win_ps", [P, 2, 512])
        xT_ps = spread_ps
        tab_ps = pre_ps[:, :, 0:4, :]
        col_ps = win_ps[:, :, :].rearrange("p s (t b) -> p s t b", b=P)

        ld_w = sem("ld_w")
        bias_turned = sem("bias_turned")
        bias_ready = sem("bias_ready")
        ld_x = [sem(f"ld_x{i}") for i in range(NODE_RING)]
        ld_edge = [sem(f"ld_edge{i}") for i in range(3)]
        padded = sem("padded")
        consts = sem("consts")
        xT_ready = sem("xT_ready")
        xT_copied = sem("xT_copied")
        xT_kept = sem("xT_kept")
        A_ready = sem("A_ready")
        A_copied = sem("A_copied")
        xT_back = sem("xT_back")
        B_ready = sem("B_ready")
        B_copied = sem("B_copied")
        A_stored = [sem(f"A_stored{i}") for i in range(NODE_RING)]
        B_stored = [sem(f"B_stored{i}") for i in range(NODE_RING)]
        prep = sem("prep")
        edge_ready = [sem(f"edge_ready{i}") for i in range(3)]
        base_ready = sem("base_ready")
        base_out = sem("base_out")
        base_in = sem("base_in")
        col_ready = sem("col_ready")
        col_copied = sem("col_copied")
        cleared = sem("cleared")
        span_ready = sem("span_ready")
        span_turned = sem("span_turned")
        flag_ready = sem("flag_ready")
        edges_done = sem("edges_done")
        idx_staged = sem("idx_staged")
        go = sem("go")
        meta_staged = sem("meta_staged")
        landed = [sem(f"landed{i}") for i in range(RING)]
        oh_ready = sem("oh_ready")
        spread_t = sem("spread_t")
        spread_sb = sem("spread_sb")
        win_loaded = [sem(f"win_loaded{i}") for i in range(2)]
        b_split = sem("b_split")
        pre_ready = sem("pre_ready")
        z_ready = sem("z_ready")
        hid_ready = sem("hid_ready")
        sum_ready = sem("sum_ready")
        sum_out = sem("sum_out")
        messages_ready = sem("messages_ready")
        sum_added = sem("sum_added")
        trash_ready = sem("trash_ready")
        table_zero = sem("table_zero")
        abs_ready = sem("abs_ready")
        abs_turned = sem("abs_turned")
        abs_copied = sem("abs_copied")
        table_clear = sem("table_clear")
        tile_step = sem("tile_step")
        tile_landed = sem("tile_landed")
        dst_turned = sem("dst_turned")
        combined = sem("combined")
        old_landed = sem("old_landed")
        scattered = sem("scattered")
        chunk_loaded = sem("chunk_loaded")
        chunk_turned = sem("chunk_turned")
        chunk_staged = sem("chunk_staged")
        chunk_ready = sem("chunk_ready")
        chunk_copied = sem("chunk_copied")
        xe_loaded = [sem(f"xe_loaded{i}") for i in range(NODE_RING)]
        sum_staged = sem("sum_staged")
        back_ready = sem("back_ready")
        y_ready = sem("y_ready")
        st_ready = sem("st_ready")
        mv_ready = sem("mv_ready")
        std_ready = sem("std_ready")
        rstd_ready = sem("rstd_ready")
        shift_ready = sem("shift_ready")
        o_ready = sem("o_ready")
        o_stored = [sem(f"o_stored{i}") for i in range(NODE_RING)]

        block = ctx.enter_context(nc.Block())

        x_main = x[0:(CHUNKS - 1) * P, :].rearrange("(c p) k -> p c k", p=P)
        out_main = out[0:(CHUNKS - 1) * P, :].rearrange("(c p) k -> p c k", p=P)
        A_rows = A_tab.rearrange("(c p) k -> p c k", p=P)
        B_rows = B_tab.rearrange("(c p) k -> p c k", p=P)
        EDGE_LOADS = DMA * (GROUPS + (1 if REST else 0))

        def chunks_in(q):
            return min(4, CHUNKS - 4 * q) if isinstance(q, int) else 4

        def columns(q):
            return bass.ds(q * 4 * P, chunks_in(q) * P)

        def load_nodes(eng, to, q, slot, signal):
            n = chunks_in(q)
            if beyond(q, QUADS - 1):
                if n > 1:
                    eng.dma_start(to[:, slot, 0:n - 1, :], x_main[:, 4 * q:4 * q + n - 1, :]).then_inc(signal, DMA)
                eng.dma_start(to[0:LAST, slot, n - 1, :], x[(CHUNKS - 1) * P:N, :]).then_inc(signal, DMA)
            else:
                eng.dma_start(to[:, slot, :, :], x_main[:, bass.ds(q * 4, 4), :]).then_inc(signal, DMA)

        def transfers(q, slot):
            extra = DMA if beyond(q, QUADS - 1) and chunks_in(q) > 1 else 0
            return rounds(q, slot, NODE_RING, DMA) + DMA + extra

        def all_stored(eng, stored, extra=0):
            for slot in range(NODE_RING):
                uses = len(range(slot, QUADS, NODE_RING))
                eng.wait_ge(stored[slot], DMA * (uses + (extra if slot == (QUADS - 1) % NODE_RING else 0)))

        def load_edges(eng, to, array, signal):
            for g in range(GROUPS):
                n = min(FULL - g * P, P)
                eng.dma_start(to[0:n, g, :], array[g * P * BLOCK:(g * P + n) * BLOCK]
                              .rearrange("(p b) -> p b", b=BLOCK)).then_inc(signal, DMA)
            if REST:
                r = FULL - g_last * P
                eng.dma_start(to[r:r + 1, g_last, 0:REST],
                              array[FULL * BLOCK:E].rearrange("(p b) -> p b", p=1)).then_inc(signal, DMA)

        def rounds(i, slot, ring, each):
            return (i - slot) * (each // ring)

        def fast_or_general(eng, fast, general):
            eng.wait_ge(flag_ready, 1)
            flag = eng.value_load(span_i[0:1, 0:1], min_val=0, max_val=NP)
            with eng.If(flag < WINDOW):
                fast()
            with eng.Else():
                general()

        @block.sync
        def _(sp):
            sp.dma_start(w1_sb[:, :, :], W1.rearrange("(h k) n -> k h n", h=2)).then_inc(ld_w, DMA)
            sp.dma_start(bias_rows[:, 0, :], b1.rearrange("(a n) -> a n", a=1)).then_inc(ld_w, DMA)
            sp.dma_start(bias_rows[:, 1, :], b2.rearrange("(a n) -> a n", a=1)).then_inc(ld_w, DMA)
            sp.dma_start(w2_sb[:, :], W2).then_inc(ld_w, DMA)
            def load_x(q, slot):
                hold(sp, xT_ready, q - NODE_RING + 1)
                load_nodes(sp, x_in, q, slot, ld_x[slot])

            for q in range(NODE_RING - 1):
                load_x(q, q)

            def x_and_A(q, slot):
                if not beyond(q + NODE_RING - 1, QUADS):
                    load_x(q + NODE_RING - 1, (slot + NODE_RING - 1) % NODE_RING)
                sp.wait_ge(A_copied, q + 1)
                n = chunks_in(q)
                sp.dma_start(A_rows[:, bass.ds(q * 4, n), :], A_sb[:, slot, 0:n, :]).then_inc(A_stored[slot], DMA)
            steps(sp, QUADS, NODE_RING, x_and_A, ahead=NODE_RING)

            sp.wait_ge(base_ready, 1)
            with nc.allow_non_contiguous_dma(reason="512 words, once"):
                sp.dma_start(base_tab.rearrange("(g p) -> p g", p=P), base_i[:, :]).then_inc(base_out, DMA)
            sp.wait_ge(base_out, DMA)
            sp.dma_start(base_row[:, :], base_tab.rearrange("(a n) -> a n", a=1)).then_inc(base_in, DMA)
            sp.wait_ge(base_in, DMA)

            def store_B(q, slot):
                sp.wait_ge(B_copied, q + 1)
                n = chunks_in(q)
                sp.dma_start(B_rows[:, bass.ds(q * 4, n), :], B_sb[:, slot, 0:n, :]).then_inc(B_stored[slot], DMA)
            steps(sp, QUADS, NODE_RING, store_B)
            all_stored(sp, B_stored)

            def load_window(s, slot):
                base = sp.value_load(base_row[0:1, bass.ds(s, 1)], min_val=0, max_val=NP - WINDOW)
                hold(sp, b_split, 4 * (s - 1))
                for h in range(2):
                    sp.dma_start(b_win[h * WINDOW:(h + 1) * WINDOW, slot, :],
                                 B_tab[bass.ds(base, WINDOW), :]).then_inc(win_loaded[slot], DMA)

            def zero_and_read_sums():
                sp.wait_ge(table_zero, 1)
                with sp.Fori(0, CHUNKS + 1) as c:
                    sp.dma_start(sum_tab[bass.ds(c * P, P), :], zero_row).then_inc(table_clear, DMA)
                sp.wait_ge(scattered, DMA * EDGE_COLS)
                with sp.Fori(0, CHUNKS) as c:
                    sp.dma_start(sum_old, sum_tab[bass.ds(c * P, P), :]).then_inc(chunk_loaded, DMA)
                    sp.wait_ge(chunk_copied, c + 1)
                    sp.sem_inc(go, 1)

            fast_or_general(sp, lambda: steps(sp, BLOCKS, 2, load_window), zero_and_read_sums)

            def load_x_again(q, slot):
                hold(sp, y_ready, q - NODE_RING + 1)
                load_nodes(sp, xe, q, slot, xe_loaded[slot])

            def store_out(q, slot):
                sp.wait_ge(o_ready, q + 1)
                n = chunks_in(q)
                if beyond(q, QUADS - 1):
                    if n > 1:
                        sp.dma_start(out_main[:, 4 * q:4 * q + n - 1, :],
                                     y[:, slot, 0:n - 1, :]).then_inc(o_stored[slot], DMA)
                    sp.dma_start(out[(CHUNKS - 1) * P:N, :], y[0:LAST, slot, n - 1, :]).then_inc(o_stored[slot], DMA)
                else:
                    sp.dma_start(out_main[:, bass.ds(q * 4, 4), :], y[:, slot, :, :]).then_inc(o_stored[slot], DMA)

            sp.wait_ge(edges_done, 1)
            for q in range(NODE_RING - 1):
                load_x_again(q, q)

            def x_and_out(q, slot):
                if not beyond(q + NODE_RING - 1, QUADS):
                    load_x_again(q + NODE_RING - 1, (slot + NODE_RING - 1) % NODE_RING)
                store_out(q, slot)
            steps(sp, QUADS, NODE_RING, x_and_out, ahead=NODE_RING)
            all_stored(sp, o_stored, extra=1 if chunks_in(QUADS - 1) > 1 else 0)

        @block.gpsimd
        def _(pool):
            nc.gpsimd.memset(ident[:, :], 0.0).then_inc(consts, 1)
            nc.gpsimd.memset(ones[:, :], 1.0).then_inc(consts, 1)
            pool.wait_ge(consts, 2)
            nc.gpsimd.affine_select(out=ident[:, :], in_=ident[:, :], compare_op=ALU.not_equal, fill=1.0,
                                    base=0, pattern=[[-1, P]], channel_multiplier=1).then_inc(consts, 1)
            nc.gpsimd.iota(window_iota[:, :], pattern=[[1, WINDOW]], base=0, channel_multiplier=0,
                           allow_small_or_imprecise_dtypes=True).then_inc(consts, 1)
            pool.wait_ge(consts, 4)
            for h in range(2):
                half = slice(h * WINDOW, (h + 1) * WINDOW)
                nc.gpsimd.tensor_copy(fold[half, :], ident[half, half]).then_inc(consts, 1)

            def keep_xT(q, slot):
                pool.wait_ge(xT_copied, q + 1)
                n = chunks_in(q)
                nc.gpsimd.tensor_copy(sumT[:, columns(q)], xT_sb[:, slot % 2, 0:n, :]
                                      .rearrange("p c n -> p (c n)")).then_inc(xT_kept, 1)
            steps(pool, QUADS, NODE_RING, keep_xT)
            all_stored(pool, A_stored)

            def gather(s, slot):
                pool.wait_ge(idx_staged, s + 1)
                hold(pool, z_ready, s - RING + 1)
                pool.sem_inc(go, 1)
                for t in range(TILES):
                    nc.gpsimd.indirect_dma_start(
                        out=rows[:, slot, t, :], out_offset=None, in_=A_tab,
                        in_offset=bass.IndirectOffsetOnAxis(ap=src_now[:, slot, t:t + 1], axis=0),
                    ).then_inc(landed[slot], DMA)

            def general():
                nc.gpsimd.iota(trash, pattern=[[0, 1]], base=NP, channel_multiplier=1,
                               allow_small_or_imprecise_dtypes=True).then_inc(trash_ready, 1)
                nc.gpsimd.affine_select(out=before, in_=ones[:, :], compare_op=ALU.is_gt, fill=0.0, base=0,
                                        pattern=[[-1, P]], channel_multiplier=1).then_inc(trash_ready, 1)
                pool.wait_ge(table_clear, DMA * (CHUNKS + 1))
                all_stored(pool, B_stored)
                with pool.Fori(0, EDGE_COLS) as t:
                    pool.wait_ge(tile_step, TILE_STEPS * t + 4)
                    pool.sem_inc(go, 1)
                    for to, table, k in ((a_rows, A_tab, 0), (b_rows, B_tab, 1)):
                        nc.gpsimd.indirect_dma_start(
                            out=to, out_offset=None, in_=table,
                            in_offset=bass.IndirectOffsetOnAxis(ap=index_now[:, k:k + 1], axis=0),
                        ).then_inc(tile_landed, DMA)
                    pool.wait_ge(tile_step, TILE_STEPS * t + INDEX_STEP)
                    pool.sem_inc(go, 1)
                    nc.gpsimd.indirect_dma_start(
                        out=sum_old, out_offset=None, in_=sum_tab,
                        in_offset=bass.IndirectOffsetOnAxis(ap=index_now[:, 2:3], axis=0),
                    ).then_inc(old_landed, DMA)
                    pool.wait_ge(tile_step, TILE_STEPS * t + TILE_STEPS)
                    pool.sem_inc(go, 1)
                    nc.gpsimd.indirect_dma_start(
                        out=sum_tab, out_offset=bass.IndirectOffsetOnAxis(ap=index_now[:, 2:3], axis=0),
                        in_=sum_new, in_offset=None).then_inc(scattered, DMA)

            fast_or_general(pool, lambda: steps(pool, BLOCKS, RING, gather), general)

            pool.wait_ge(edges_done, 1)

            def stage_sum(q, slot):
                hold(pool, back_ready, q - 1)
                n = chunks_in(q)
                nc.gpsimd.tensor_copy(sum_now[:, slot % 2, 0:n, :].rearrange("p c n -> p (c n)"),
                                      sumT[:, columns(q)]).then_inc(sum_staged, 1)
            steps(pool, QUADS, NODE_RING, stage_sum)

        @block.scalar
        def _(act):
            act.wait_ge(padded, 3)
            load_edges(act, src_i, src, ld_edge[1])
            load_edges(act, dst_i, dst, ld_edge[0])
            load_edges(act, w_f, edge_weight, ld_edge[2])

            act.wait_ge(bias_turned, 1)
            nc.scalar.copy(bias_wide[:, :, :], win_ps[:, 0, 0:2 * D].rearrange("p (b n) -> p b n", b=2)
                           ).then_inc(bias_ready, 1)

            def copy_xT(q, slot):
                act.wait_ge(xT_ready, q + 1)
                hold(act, A_ready, q - 1)
                hold(act, xT_kept, q - 1)
                n = chunks_in(q)
                nc.scalar.copy(xT_sb[:, slot % 2, 0:n, :], xT_ps[:, slot % 2, 0:n, :]).then_inc(xT_copied, 1)

            copy_xT(0, 0)

            def first_table(q, slot):
                if not beyond(q + 1, QUADS):
                    copy_xT(q + 1, (slot + 1) % NODE_RING)
                act.wait_ge(A_ready, q + 1)
                hold(act, A_stored[slot], rounds(q, slot, NODE_RING, DMA))
                n = chunks_in(q)
                nc.scalar.copy(A_sb[:, slot, 0:n, :], tab_ps[:, slot % 2, 0:n, :]).then_inc(A_copied, 1)
            steps(act, QUADS, NODE_RING, first_table, ahead=2)

            def xT_again(q, slot):
                act.wait_ge(A_ready, QUADS)
                act.wait_ge(xT_kept, QUADS)
                hold(act, B_ready, q - 1)
                n = chunks_in(q)
                nc.scalar.copy(xT_sb[:, slot % 2, 0:n, :], sumT[:, columns(q)]
                               .rearrange("p (c n) -> p c n", c=n)).then_inc(xT_back, 1)
            steps(act, QUADS, NODE_RING, xT_again)

            def copy_spread(s, slot):
                act.wait_ge(spread_t, s + 1)
                hold(act, pre_ready, s - 1)
                hold(act, sum_out, 2 * (s - RING + 1))
                nc.scalar.activation(spread[:, slot % 2, :, :], spread_ps[:, slot % 2, :, :], ACT.Copy,
                                     accum_out=count[:, slot, :]).then_inc(spread_sb, 1)

            def copy_sums(s, slot):
                act.wait_ge(sum_ready, s + 1)
                hold(act, messages_ready, s - 1)
                nc.scalar.copy(win_sum[:, slot % 2, :], win_ps[:, slot % 2, 0:WINDOW]).then_inc(sum_out, 1)
                nc.scalar.activation(fold_count[:, slot % 2, :], fold[:, :], ACT.Copy,
                                     scale=count[:, slot, :]).then_inc(sum_out, 1)


            def hidden(s, slot):
                if not beyond(-s, 0):
                    copy_sums(s - 1, (slot - 1) % RING)
                act.wait_ge(z_ready, s + 1)
                here = hid[:, slot % 2, :, :]
                nc.scalar.activation(here, here, ACT.Relu).then_inc(hid_ready, 1)
                if not beyond(s + 2, BLOCKS):
                    copy_spread(s + 2, (slot + 2) % RING)

            def fast():
                copy_spread(0, 0)
                copy_spread(1, 1)
                steps(act, BLOCKS, RING, hidden, ahead=2)
                copy_sums(BLOCKS - 1, (BLOCKS - 1) % RING)

            fast_or_general(act, fast, lambda: act.wait_ge(edges_done, 1))

            act.wait_ge(edges_done, 1)

            def stdev(q, slot):
                act.wait_ge(mv_ready, q + 1)
                hold(act, rstd_ready, q - 1)
                n = chunks_in(q)
                nc.scalar.activation(std[:, slot % 2, 0:n], mv[:, slot % 2, 0:n, 1], ACT.Sqrt,
                                     bias=eps_col[:, 0:1], scale=1.0).then_inc(std_ready, 1)

            def scale(q, slot):
                act.wait_ge(shift_ready, q + 1)
                for c in range(chunks_in(q)):
                    last = nc.scalar.activation(y[:, slot, c, :], y[:, slot, c, :], ACT.Identity,
                                                scale=rstd[:, slot % 2, c:c + 1], bias=shift[:, slot % 2, c:c + 1])
                last.then_inc(o_ready, 1)

            def stdev_and_scale(q, slot):
                stdev(q, slot)
                if not beyond(-q, 0):
                    scale(q - 1, (slot - 1) % NODE_RING)
            steps(act, QUADS, NODE_RING, stdev_and_scale)
            scale(QUADS - 1, (QUADS - 1) % NODE_RING)

        @block.vector
        def _(dve):
            nc.vector.memset(dst_i[:, g_last, :], -1).then_inc(padded, 1)
            nc.vector.memset(src_f[:, g_last, :], 0.0).then_inc(padded, 1)
            nc.vector.memset(w_f[:, g_last, :], 0.0).then_inc(padded, 1)
            nc.vector.memset(zeros[:, :], 0.0).then_inc(padded, 1)
            nc.vector.memset(eps_col[:, :], EPS).then_inc(padded, 1)

            done = [0]

            def step(instruction):
                done[0] += 1
                instruction.then_inc(prep, 1)
                dve.wait_ge(prep, done[0])

            dve.wait_ge(ld_edge[1], EDGE_LOADS)
            for g in range(GROUPS):
                nc.vector.tensor_copy(src_f[:, g, :], src_i[:, g, :]).then_inc(edge_ready[1], 1)
            dve.wait_ge(ld_edge[0], EDGE_LOADS)
            for g in range(GROUPS):
                step(nc.vector.tensor_copy(dst_f[:, g, :], dst_i[:, g, :]))
                if g == g_last:
                    step(nc.vector.tensor_scalar(min_tmp, dst_f[:, g, :], 0.0, float(2 * NP),
                                                 ALU.is_lt, ALU.mult))
                    step(nc.vector.tensor_tensor(min_tmp, min_tmp, dst_f[:, g, :], ALU.add))
                    step(nc.vector.tensor_reduce(lo[:, g:g + 1], min_tmp, AX.X, ALU.min))
                else:
                    step(nc.vector.tensor_reduce(lo[:, g:g + 1], dst_f[:, g, :], AX.X, ALU.min))
                step(nc.vector.tensor_reduce(hi[:, g:g + 1], dst_f[:, g, :], AX.X, ALU.max))
            step(nc.vector.tensor_scalar(base_f[:, :], lo[:, :], float(NP - WINDOW), None, ALU.min))
            nc.vector.tensor_copy(base_i[:, :], base_f[:, :]).then_inc(base_ready, 1)
            step(nc.vector.tensor_tensor(span[:, :], hi[:, :], base_f[:, :], ALU.subtract))
            nc.vector.tensor_reduce(span_p[:, :], span[:, :], AX.X, ALU.max).then_inc(span_ready, 1)
            for g in range(GROUPS):
                nc.vector.tensor_scalar(dst_f[:, g, :], dst_f[:, g, :], base_f[:, g:g + 1], None,
                                        ALU.subtract).then_inc(edge_ready[0], 1)

            dve.wait_ge(span_turned, 1)
            step(nc.vector.tensor_reduce(span_one[:, :], win_ps[0:1, 0, 0:P], AX.X, ALU.max))
            nc.vector.tensor_copy(span_i[:, :], span_one[:, :]).then_inc(flag_ready, 1)

            def copy_columns(some):
                for j in some:
                    a, g, h = COLS[j]
                    n = min(BLOCKS - g * P, P)
                    dve.wait_ge(col_ready, j + 1)
                    to = src_col if a == 1 else meta[:, :, 0 if a == 0 else 1, :]
                    nc.vector.tensor_copy(to[:, g * P:g * P + n, h * HALF:(h + 1) * HALF],
                                          col_ps[:, j % 2, :, 0:n].rearrange("p t b -> p b t")).then_inc(col_copied, 1)

            copy_columns(SRC_COLS)

            def stage_index(s, slot):
                nc.vector.tensor_copy(src_now[:, slot, :], src_col[:, bass.ds(s, 1), :]
                                      .rearrange("p a t -> p (a t)")).then_inc(idx_staged, 1)

            def stage_meta(s, slot):
                hold(dve, z_ready, s - RING + 1)
                nc.vector.tensor_copy(meta_now[:, slot, :, :], meta[:, bass.ds(s, 1), :, :]
                                      .rearrange("p a m t -> p (a m) t")).then_inc(meta_staged, 1)

            def one_hots(s, slot):
                dve.wait_ge(meta_staged, s + 1)
                hold(dve, sum_ready, s - RING + 1)
                for t in range(TILES):
                    last = nc.vector.tensor_scalar(onehot[:, slot, t % HALF, t // HALF, :], window_iota[:, :],
                                                   meta_now[:, slot, 0, t:t + 1], None, ALU.is_equal)
                last.then_inc(oh_ready, 1)

            def pre_hidden(s, slot):
                dve.wait_ge(pre_ready, s + 1)
                dve.wait_ge(landed[slot], rounds(s, slot, RING, DMA * TILES) + DMA * TILES)
                hold(dve, sum_ready, s - 1)
                for t in range(TILES):
                    last = nc.vector.scalar_tensor_tensor(
                        out=hid[:, slot % 2, t, :], in0=rows[:, slot, t, :], scalar=meta_now[:, slot, 1, t:t + 1],
                        in1=pre_ps[:, slot % 2, t, :], op0=ALU.mult, op1=ALU.add)
                last.then_inc(z_ready, 1)

            def add_sums(s, slot):
                base = dve.value_load(base_row[0:1, bass.ds(s, 1)], min_val=0, max_val=NP - WINDOW)
                dve.wait_ge(messages_ready, s + 1)
                hold(dve, sum_added, s)
                to = sumT[:, bass.ds(base, WINDOW)]
                nc.vector.tensor_tensor(to, to, win_ps[:, slot, WINDOW:2 * WINDOW], ALU.add).then_inc(sum_added, 1)

            def split_window(s, slot, part):
                if part == 0:
                    dve.wait_ge(win_loaded[slot], rounds(s, slot, 2, 2 * DMA) + 2 * DMA)
                    hold(dve, pre_ready, s - 1)
                else:
                    dve.wait_ge(b_split, 4 * s + part)
                if part % 2 == 0:
                    left = b_win if part == 0 else b_left
                    nc.vector.tensor_copy(b_part[:, slot, part // 2, :], left[:, slot, :]).then_inc(b_split, 1)
                else:
                    left, to = (b_win[:, slot, :], b_left[:, slot, :]) if part == 1 else \
                        (b_left[:, slot, :], b_part[:, slot, 2, :])
                    nc.vector.tensor_tensor(to, left, b_part[:, slot, part // 2, :],
                                            ALU.subtract).then_inc(b_split, 1)

            def edges(s, slot):
                if not beyond(s + RING - 1, BLOCKS):
                    stage_index(s + RING - 1, (slot + RING - 1) % RING)
                ahead = not beyond(s + 2, BLOCKS)
                if ahead:
                    stage_meta(s + 2, (slot + 2) % RING)
                    split_window(s + 2, slot % 2, 0)
                    one_hots(s + 2, (slot + 2) % RING)
                    split_window(s + 2, slot % 2, 1)
                pre_hidden(s, slot)
                if ahead:
                    split_window(s + 2, slot % 2, 2)
                if not beyond(-s, 0):
                    add_sums(s - 1, (slot - 1) % 2)
                if ahead:
                    split_window(s + 2, slot % 2, 3)
            def second_table(q, slot, clear=False):
                dve.wait_ge(xT_back, q + 1)
                dve.wait_ge(B_ready, q + 1)
                hold(dve, B_stored[slot], rounds(q, slot, NODE_RING, DMA))
                for c in range(chunks_in(q)):
                    last = nc.vector.tensor_tensor(B_sb[:, slot, c, :], bias_wide[:, 0, :], tab_ps[:, slot % 2, c, :],
                                                   ALU.add)
                last.then_inc(B_copied, 1)
                if clear:
                    nc.vector.tensor_copy(sumT[:, columns(q)], zeros[:, 0:chunks_in(q) * P]).then_inc(cleared, 1)

            def fast():
                dve.wait_ge(col_copied, len(SRC_COLS))
                for s in range(RING - 1):
                    stage_index(s, s)
                copy_columns(OTHER_COLS)
                dve.wait_ge(col_copied, len(COLS))
                for s in range(2):
                    stage_meta(s, s)
                    one_hots(s, s)
                dve.wait_ge(bias_ready, 1)
                steps(dve, QUADS, NODE_RING, lambda q, slot: second_table(q, slot, clear=True))
                dve.wait_ge(cleared, QUADS)
                all_stored(dve, B_stored)
                dve.wait_ge(base_in, DMA)
                for s in range(2):
                    for part in range(4):
                        split_window(s, s, part)
                steps(dve, BLOCKS, RING, edges, ahead=RING - 1)
                add_sums(BLOCKS - 1, (BLOCKS - 1) % 2)
                dve.wait_ge(sum_added, BLOCKS)
                dve.sem_inc(edges_done, 1)

            def general():
                copy_columns(OTHER_COLS)
                dve.wait_ge(col_copied, len(COLS))
                dve.wait_ge(bias_ready, 1)
                steps(dve, QUADS, NODE_RING, second_table)
                dve.wait_ge(xT_kept, QUADS)
                all_stored(dve, A_stored)
                nc.vector.memset(zero_row, 0.0).then_inc(table_zero, 1)
                nc.vector.memset(hid_one[:, D:D + 1], 1.0).then_inc(abs_copied, 1)
                for g in range(GROUPS):
                    nc.vector.tensor_scalar(dst_f[:, g, :], dst_f[:, g, :], base_f[:, g:g + 1], None,
                                            ALU.add).then_inc(abs_ready, 1)
                nc.vector.tensor_copy(w_cols.rearrange("p (b t) -> p b t", t=TILES),
                                      meta[:, :, 1, :]).then_inc(abs_copied, 1)
                for j in range(2 * GROUPS):
                    g, h = j // 2, j % 2
                    n = min(BLOCKS - g * P, P)
                    dve.wait_ge(abs_turned, j + 1)
                    nc.vector.tensor_copy(dst_cols.rearrange("p (b t) -> p b t", t=TILES)
                                          [:, g * P:g * P + n, h * HALF:(h + 1) * HALF],
                                          col_ps[:, j % 2, :, 0:n].rearrange("p t b -> p b t")).then_inc(abs_copied, 1)
                dve.wait_ge(abs_copied, 2 * GROUPS + 2)
                dve.wait_ge(trash_ready, 2)

                with dve.Fori(0, EDGE_COLS) as t:
                    taken = [0]

                    def then(instruction):
                        taken[0] += 1
                        instruction.then_inc(tile_step, 1)
                        dve.wait_ge(tile_step, TILE_STEPS * t + taken[0])

                    then(nc.vector.tensor_copy(dst_now, dst_cols[:, bass.ds(t, 1)]))
                    then(nc.vector.tensor_copy(w_now, w_cols[:, bass.ds(t, 1)]))
                    then(nc.vector.tensor_copy(index_now[:, 0:1], src_cols[:, bass.ds(t, 1)]))
                    then(nc.vector.tensor_scalar(index_now[:, 1:2], dst_now, 0.0, None, ALU.max))
                    then(nc.vector.tensor_scalar(dst_wide, ones[:, :], dst_now, None, ALU.mult))
                    dve.wait_ge(dst_turned, t + 1)
                    then(nc.vector.tensor_scalar(equal, spread_ps[:, 0, 0, :], dst_now, None, ALU.is_equal))
                    then(nc.vector.tensor_tensor(earlier, equal, before, ALU.mult))
                    then(nc.vector.tensor_reduce(n_before, earlier, AX.X, ALU.add))
                    then(nc.vector.tensor_scalar(first, n_before, 0.5, None, ALU.is_lt))
                    then(nc.vector.tensor_scalar(is_edge, dst_now, 0.0, None, ALU.is_ge))
                    then(nc.vector.tensor_tensor(first, first, is_edge, ALU.mult))
                    then(nc.vector.tensor_tensor(at_now, dst_now, trash, ALU.subtract))
                    then(nc.vector.tensor_tensor(at_now, at_now, first, ALU.mult))
                    then(nc.vector.tensor_tensor(index_now[:, 2:3], at_now, trash, ALU.add))
                    assert taken[0] == INDEX_STEP
                    dve.wait_ge(tile_landed, 2 * DMA * t + 2 * DMA)
                    then(nc.vector.scalar_tensor_tensor(out=hid_one[:, 0:D], in0=a_rows, scalar=w_now, in1=b_rows,
                                                        op0=ALU.mult, op1=ALU.add))
                    then(nc.vector.tensor_scalar(hid_one[:, 0:D], hid_one[:, 0:D], 0.0, None, ALU.max))
                    assert taken[0] == INDEX_STEP + 2
                    dve.wait_ge(combined, t + 1)
                    dve.wait_ge(old_landed, DMA * t + DMA)
                    then(nc.vector.tensor_tensor(sum_new, sum_old, win_ps[:, 0, 0:D + 1], ALU.add))
                    assert taken[0] == TILE_STEPS
                    dve.wait_ge(scattered, DMA * t + DMA)

                with dve.Fori(0, CHUNKS) as c:
                    dve.wait_ge(chunk_turned, c + 1)
                    nc.vector.tensor_copy(hid_T, spread_ps[:, 0, 0, :]).then_inc(chunk_staged, 1)
                    nc.vector.tensor_copy(degree_T, spread_ps[0:1, 0, 1, :]).then_inc(chunk_staged, 1)
                    dve.wait_ge(chunk_ready, c + 1)
                    nc.vector.tensor_copy(sumT[:, bass.ds(c * P, P)], win_ps[:, 0, 0:P]).then_inc(chunk_copied, 1)
                dve.wait_ge(chunk_copied, CHUNKS)
                dve.sem_inc(edges_done, 1)

            fast_or_general(dve, fast, general)

            def add_x(q, slot):
                dve.wait_ge(back_ready, q + 1)
                dve.wait_ge(xe_loaded[slot], transfers(q, slot))
                hold(dve, o_stored[slot], rounds(q, slot, NODE_RING, DMA))
                n = chunks_in(q)
                nc.vector.tensor_tensor(y[:, slot, 0:n, :], xe[:, slot, 0:n, :],
                                        win_ps[:, slot % 2, 0:n * D].rearrange("p (c d) -> p c d", c=n),
                                        ALU.add).then_inc(y_ready, 1)

            def rstd_and_shift(q, slot):
                dve.wait_ge(std_ready, q + 1)
                hold(dve, o_ready, q - 1)
                n = chunks_in(q)
                nc.vector.reciprocal(rstd[:, slot, 0:n], std[:, slot, 0:n]).then_inc(rstd_ready, 1)
                dve.wait_ge(rstd_ready, q + 1)
                nc.vector.scalar_tensor_tensor(out=shift[:, slot, 0:n], in0=mv[:, slot, 0:n, 0], scalar=-1.0,
                                               in1=rstd[:, slot, 0:n], op0=ALU.mult, op1=ALU.mult
                                               ).then_inc(shift_ready, 1)

            def norm(q, slot):
                n = chunks_in(q)
                add_x(q, slot)
                dve.wait_ge(y_ready, q + 1)
                for c in range(n):
                    last = nc.vector.bn_stats(stats[:, slot % 2, c, :], y[:, slot, c, :])
                last.then_inc(st_ready, 1)
                if not beyond(-q, 0):
                    rstd_and_shift(q - 1, (slot - 1) % 2)
                dve.wait_ge(st_ready, q + 1)
                dve.sem_inc(go, 1)
                for c in range(n):
                    last = nc.vector.bn_aggr(mv[:, slot % 2, c, :], stats[:, slot % 2, c, :])
                last.then_inc(mv_ready, 1)
            steps(dve, QUADS, NODE_RING, norm)
            rstd_and_shift(QUADS - 1, (QUADS - 1) % 2)

        @block.tensor
        def _(pe):
            pe.wait_ge(consts, 6)
            pe.wait_ge(ld_w, 4 * DMA)

            nc.tensor.matmul(win_ps[:, 0, 0:2 * D], ones[0:1, :], bias_rows[:, :, :].rearrange("p b n -> p (b n)"),
                             start=True, stop=True).then_inc(bias_turned, 1)

            def transpose_x(q, slot):
                pe.wait_ge(ld_x[slot], transfers(q, slot))
                hold(pe, xT_copied, q - 1)
                for c in range(chunks_in(q)):
                    last = nc.tensor.transpose(xT_ps[:, slot % 2, c, :], x_in[:, slot, c, :], ident[:, :])
                last.then_inc(xT_ready, 1)

            def product(q, slot, half, xT_there, copied, ready):
                pe.wait_ge(xT_there, q + 1)
                hold(pe, copied, q - 1)
                for c in range(chunks_in(q)):
                    last = nc.tensor.matmul(tab_ps[:, slot % 2, c, :], xT_sb[:, slot % 2, c, :], w1_sb[:, half, :],
                                            start=True, stop=True)
                last.then_inc(ready, 1)

            def first_table(q, slot):
                if not beyond(q + 1, QUADS):
                    transpose_x(q + 1, (slot + 1) % NODE_RING)
                product(q, slot, 0, xT_copied, A_copied, A_ready)

            def turn_columns(some):
                for j in some:
                    a, g, h = COLS[j]
                    n = min(BLOCKS - g * P, P)
                    pe.wait_ge(edge_ready[a] if a < 2 else ld_edge[2], g + 1 if a < 2 else EDGE_LOADS)
                    hold(pe, col_copied, j - 1)
                    for t in range(HALF):
                        at = (h * HALF + t) * P
                        last = nc.tensor.transpose(col_ps[:, j % 2, t, 0:n], arrays[0:n, a, g, at:at + P],
                                                   ident[0:n, 0:n])
                    last.then_inc(col_ready, 1)

            transpose_x(0, 0)
            steps(pe, SPLIT, NODE_RING, first_table)
            pe.wait_ge(bias_ready, 1)
            pe.wait_ge(span_ready, 1)
            nc.tensor.transpose(win_ps[0:1, 0, 0:P], span_p[:, :], ident[:, :]).then_inc(span_turned, 1)
            pe.wait_ge(flag_ready, 1)
            turn_columns(SRC_COLS)
            steps(pe, QUADS, NODE_RING, first_table, ahead=2, first=SPLIT)
            turn_columns(OTHER_COLS)
            pe.wait_ge(A_copied, QUADS)
            steps(pe, QUADS, NODE_RING, lambda q, slot: product(q, slot, 1, xT_back, B_copied, B_ready))

            def spread_one_hots(s, slot):
                pe.wait_ge(oh_ready, s + 1)
                hold(pe, spread_sb, s - 1)
                for t in range(HALF):
                    last = nc.tensor.transpose(spread_ps[:, slot % 2, t, :], onehot[:, slot, t, :, :]
                                               .rearrange("p h w -> p (h w)"), ident[:, :])
                last.then_inc(spread_t, 1)

            def spread_window(s, slot):
                pe.wait_ge(spread_sb, s + 1)
                pe.wait_ge(b_split, 4 * s + 4)
                hold(pe, z_ready, s - 1)
                for t in range(TILES):
                    h = t // HALF
                    half = slice(h * WINDOW, (h + 1) * WINDOW)
                    for part in range(3):
                        last = nc.tensor.matmul(pre_ps[:, slot, t, :], spread[half, slot, t % HALF, :],
                                                b_part[half, slot, part, :], start=(part == 0), stop=(part == 2))
                last.then_inc(pre_ready, 1)

            def sum_edges(s, slot):
                pe.wait_ge(hid_ready, s + 1)
                hold(pe, sum_out, 2 * (s - 1))
                ring_slot, slot = slot, slot % 2
                for t in range(TILES):
                    last = nc.tensor.matmul(win_ps[:, slot, 0:WINDOW], hid[:, slot, t, :],
                                            onehot[:, ring_slot, t % HALF, t // HALF, :],
                                            start=(t == 0), stop=(t == TILES - 1))
                last.then_inc(sum_ready, 1)

            def messages(s, slot):
                pe.wait_ge(sum_out, 2 * s + 2)
                hold(pe, sum_added, s - 1)
                to = win_ps[:, slot, WINDOW:2 * WINDOW]
                nc.tensor.matmul(to, w2_sb[:, :], win_sum[:, slot, :], start=True, stop=False)
                nc.tensor.matmul(to, bias_wide[:, 1, :], fold_count[:, slot, :], start=False,
                                 stop=True).then_inc(messages_ready, 1)

            def edges(s, slot):
                if not beyond(s + 2, BLOCKS):
                    spread_one_hots(s + 2, (slot + 2) % RING)
                if not beyond(s + 1, BLOCKS):
                    spread_window(s + 1, (slot + 1) % 2)
                if not beyond(-s, 0):
                    messages(s - 1, (slot - 1) % 2)
                sum_edges(s, slot)

            def fast():
                spread_one_hots(0, 0)
                spread_one_hots(1, 1)
                spread_window(0, 0)
                steps(pe, BLOCKS, RING, edges, ahead=2)
                messages(BLOCKS - 1, (BLOCKS - 1) % 2)

            def general():
                for j in range(2 * GROUPS):
                    g, h = j // 2, j % 2
                    n = min(BLOCKS - g * P, P)
                    pe.wait_ge(abs_ready, g + 1)
                    hold(pe, abs_copied, j + 1)
                    for t in range(HALF):
                        at = (h * HALF + t) * P
                        last = nc.tensor.transpose(col_ps[:, j % 2, t, 0:n], dst_f[0:n, g, at:at + P],
                                                   ident[0:n, 0:n])
                    last.then_inc(abs_turned, 1)
                with pe.Fori(0, EDGE_COLS) as t:
                    pe.wait_ge(tile_step, TILE_STEPS * t + 5)
                    nc.tensor.transpose(spread_ps[:, 0, 0, :], dst_wide, ident[:, :]).then_inc(dst_turned, 1)
                    pe.wait_ge(tile_step, TILE_STEPS * t + INDEX_STEP + 2)
                    nc.tensor.matmul(win_ps[:, 0, 0:D + 1], equal, hid_one, start=True,
                                     stop=True).then_inc(combined, 1)
                with pe.Fori(0, CHUNKS) as c:
                    pe.wait_ge(chunk_loaded, DMA * c + DMA)
                    nc.tensor.transpose(spread_ps[:, 0, 0, :], sum_old[:, 0:D], ident[:, :])
                    nc.tensor.transpose(spread_ps[0:1, 0, 1, :], sum_old[:, D:D + 1],
                                        ident[:, :]).then_inc(chunk_turned, 1)
                    pe.wait_ge(chunk_staged, 2 * c + 2)
                    nc.tensor.matmul(win_ps[:, 0, 0:P], w2_sb[:, :], hid_T, start=True, stop=False)
                    nc.tensor.matmul(win_ps[:, 0, 0:P], bias_rows[:, 1, :], degree_T, start=False,
                                     stop=True).then_inc(chunk_ready, 1)

            fast_or_general(pe, fast, general)

            def turn_back(q, slot):
                pe.wait_ge(sum_staged, q + 1)
                hold(pe, y_ready, q - 1)
                for c in range(chunks_in(q)):
                    last = nc.tensor.transpose(win_ps[:, slot % 2, c * D:(c + 1) * D], sum_now[:, slot % 2, c, :],
                                               ident[:, :])
                last.then_inc(back_ready, 1)
            steps(pe, QUADS, NODE_RING, turn_back)


_INS = ['x', 'src', 'dst', 'edge_weight', 'L0_gnn_W1', 'L0_gnn_b1', 'L0_gnn_W2', 'L0_gnn_b2']


def kernel(**inputs):
    import numpy as _np
    import concourse.bacc as _bacc
    from concourse import mybir as _mybir
    from concourse.bass_utils import run_bass_kernel_spmd as _run

    nc = _bacc.Bacc("TRN2", target_bir_lowering=False, num_devices=1)
    arrays, args = {}, []
    for name in _INS:
        a = _np.ascontiguousarray(inputs[name])
        arrays[f"in_{name}_dram"] = a
        args.append(nc.dram_tensor(f"in_{name}_dram", a.shape, _mybir.dt.from_np(a.dtype), kind="ExternalInput").ap())
    args.append(nc.dram_tensor("out_0_dram", arrays["in_x_dram"].shape, F32, kind="ExternalOutput").ap())
    gnn_kernel(nc, *args)
    r = _run(nc, [arrays], core_ids=[0])
    return r.results[0]["out_0_dram"]
```

```python
from contextlib import ExitStack

import concourse.bass as bass
from concourse import mybir

F32 = mybir.dt.float32
I32 = mybir.dt.int32
BF16 = mybir.dt.bfloat16
ALU = mybir.AluOpType
ACT = mybir.ActivationFunctionType
AX = mybir.AxisListType

P = 128
TILES = 8
BLOCK = TILES * P
WINDOW = 64
ROWS_RING = 8
RING = 4
NODE_RING = 4
EPS = 1e-5
DMA = 16


def steps(eng, count, ring, body, ahead=0, first=0):
    start = -(-first // ring) * ring + ring
    end = start + (count - ahead - start) // ring * ring
    if end <= start:
        start = end = first
    for i in range(first, start):
        body(i, i % ring)
    if end > start:
        with eng.Fori(start, end - ring + 1, ring) as i:
            for slot in range(ring):
                body(i + slot, slot)
    for i in range(end, count):
        body(i, i % ring)


def hold(eng, semaphore, value):
    if not isinstance(value, int) or value > 0:
        eng.wait_ge(semaphore, value)


def beyond(i, count):
    return isinstance(i, int) and i >= count


def opens(i, firsts):
    return isinstance(i, int) and i in firsts


def gnn_kernel(nc, x, src, dst, edge_weight, W1, b1, W2, b2, out):
    N, D = x.shape
    E = src.shape[0]
    assert D == P and W1.shape[0] == 2 * D
    CHUNKS = -(-N // P)
    QUADS = -(-CHUNKS // 4)
    SPLIT = QUADS // 8 * 5
    LAST = N - (CHUNKS - 1) * P
    NP = CHUNKS * P
    BLOCKS = -(-E // BLOCK)
    GROUPS = -(-BLOCKS // P)
    FULL = E // BLOCK
    REST = E - FULL * BLOCK
    HALF = TILES // 2
    CUTS = []
    for cut in (BLOCKS * 5 // 8 // ROWS_RING * ROWS_RING, (BLOCKS // ROWS_RING - 6) * ROWS_RING):
        quads = (cut - RING) * BLOCK * N // E // (4 * P)
        if quads > 0 and cut > (CUTS[-1][0] if CUTS else ROWS_RING):
            CUTS.append((cut, quads))
    g_last = GROUPS - 1
    TILE_STEPS, INDEX_STEP = 17, 14
    COLS = [(a, g, h) for a in (1, 0, 2) for g in range(GROUPS) for h in range(2)]
    SRC_COLS, OTHER_COLS = range(2 * GROUPS), range(2 * GROUPS, 6 * GROUPS)

    with ExitStack() as ctx:
        def sb(name, shape, dt=F32):
            return ctx.enter_context(nc.sbuf_tensor(name, shape, dt))

        def ps(name, shape, dt=F32):
            return ctx.enter_context(nc.psum_tensor(name, shape, dt))

        def sem(name):
            return ctx.enter_context(nc.semaphore(name))

        A_tab = nc.dram_tensor("A_tab", (NP, D), F32, kind="Internal").ap()
        B_tab = nc.dram_tensor("B_tab", (NP, D), F32, kind="Internal").ap()
        sum_tab = nc.dram_tensor("sum_tab", (NP + P, D + 1), F32, kind="Internal").ap()
        base_tab = nc.dram_tensor("base_tab", (GROUPS * P,), I32, kind="Internal").ap()

        rows = sb("rows", [P, ROWS_RING, TILES, D])
        ident = sb("ident", [P, P])
        ones = sb("ones", [P, P])
        window_iota = sb("window_iota", [P, WINDOW])
        eps_col = sb("eps_col", [P, 1])
        zeros = sb("zeros", [P, 4 * P])
        w1_sb = sb("w1_sb", [P, 2, D])
        w2_sb = sb("w2_sb", [P, D])
        bias_rows = sb("bias_rows", [1, 2, D])
        bias_wide = sb("bias_wide", [P, 2, D])
        sumT = sb("sumT", [P, NP])
        ROOM = max(GROUPS, -(-(RING * TILES * WINDOW + NODE_RING * 4 * D) // BLOCK))
        arrays = sb("arrays", [P, 3, ROOM, BLOCK])
        dst_f, src_f, w_f = (arrays[:, a, :, :] for a in range(3))
        dst_i, src_i = dst_f.bitcast(I32), src_f.bitcast(I32)
        src_col = sb("src_col", [P, BLOCKS, TILES], I32)
        meta = sb("meta", [P, BLOCKS, 2, TILES])
        lo = sb("lo", [P, GROUPS])
        hi = sb("hi", [P, GROUPS])
        base_f = sb("base_f", [P, GROUPS])
        base_i = sb("base_i", [P, GROUPS], I32)
        span = sb("span", [P, GROUPS])
        block_no = sb("block_no", [P, GROUPS])
        lowest = sb("lowest", [P, GROUPS])
        lowest_by = sb("lowest_by", [P, len(CUTS) + 1, GROUPS])
        span_p = sb("span_p", [P, 2])
        base_row = sb("base_row", [1, GROUPS * P], I32)
        span_one = sb("span_one", [1, 2])
        span_i = sb("span_i", [1, 2], I32)
        x_in = rows[:, 0:NODE_RING, 0:4, :]
        A_sb = rows[:, 0:NODE_RING, 4:8, :]
        xT_sb = sb("xT_sb", [P, 2, 4, P])
        src_now = sb("src_now", [P, ROWS_RING, TILES], I32)
        meta_now = sb("meta_now", [P, RING, 2, TILES])
        onehot = arrays[:, 1, :, :].rearrange("p g b -> p (g b)")[:, 0:RING * TILES * WINDOW] \
            .rearrange("p (s t h w) -> p s t h w", s=RING, t=HALF, h=2)
        spread = sb("spread", [P, 2, HALF, P], BF16)
        b_part = sb("b_part", [P, 2, 3, D], BF16)
        b_left = sb("b_left", [P, 2, D])
        count = sb("count", [P, RING, 1])
        fold = sb("fold", [P, WINDOW])
        b_win = sb("b_win", [P, 2, D])
        fold_count = sb("fold_count", [P, 2, WINDOW])
        win_sum = sb("win_sum", [P, 2, WINDOW])
        hid = arrays[:, 2, :, :].rearrange("p g b -> p (g b)")[:, 0:2 * TILES * D] \
            .rearrange("p (s t d) -> p s t d", s=2, t=TILES)
        B_sb = hid[:, :, :, :].rearrange("p s (h c) d -> p (s h) c d", c=4)
        xe = arrays[:, 2, :, :].rearrange("p g b -> p (g b)")[:, 2 * TILES * D:2 * TILES * D + NODE_RING * 4 * D] \
            .rearrange("p (s c d) -> p s c d", s=NODE_RING, c=4)
        y = arrays[:, 1, :, :].rearrange("p g b -> p (g b)")[:, RING * TILES * WINDOW:
                                                             RING * TILES * WINDOW + NODE_RING * 4 * D] \
            .rearrange("p (s c d) -> p s c d", s=NODE_RING, c=4)
        sum_now = xT_sb
        stats = sb("stats", [P, 2, 4, 6])
        mv = sb("mv", [P, 2, 4, 2])
        std = sb("std", [P, 2, 4])
        rstd = sb("rstd", [P, 2, 4])
        shift = sb("shift", [P, 2, 4])
        min_tmp = meta[:, 0:BLOCK // (2 * TILES), :, :].rearrange("p b m t -> p (b m t)")

        EDGE_COLS = BLOCKS * TILES
        src_cols = src_col[:, :, :].rearrange("p b t -> p (b t)")
        dst_cols = sumT[:, 0:EDGE_COLS]
        w_cols = sumT[:, EDGE_COLS:2 * EDGE_COLS]
        tile_buf = rows[:, :, :, :].rearrange("p r t d -> p (r t d)")
        a_rows, b_rows, equal, earlier, dst_wide, before = (tile_buf[:, i * D:(i + 1) * D] for i in range(6))
        hid_one, sum_old, sum_new, zero_row = (tile_buf[:, 1024 + 256 * i:1024 + 256 * i + D + 1] for i in range(4))
        cols = tile_buf[:, 2048:2056]
        dst_now, w_now, first, is_edge, at_now, trash, n_before, dst_safe = (cols[:, i:i + 1] for i in range(8))
        hid_T = tile_buf[:, 2176:2304]
        degree_T = tile_buf[0:1, 2304:2432]
        index_now = sb("index_now", [P, 3], I32)

        spread_ps = ps("spread_ps", [P, 2, HALF, P])
        pre_ps = ps("pre_ps", [P, 2, TILES, D])
        win_ps = ps("win_ps", [P, 2, 512])
        xT_ps = spread_ps
        tab_ps = pre_ps[:, :, 0:4, :]
        col_ps = win_ps[:, :, :].rearrange("p s (t b) -> p s t b", b=P)

        ld_w = sem("ld_w")
        bias_turned = sem("bias_turned")
        bias_ready = sem("bias_ready")
        ld_x = [sem(f"ld_x{i}") for i in range(NODE_RING)]
        ld_edge = [sem(f"ld_edge{i}") for i in range(3)]
        padded = sem("padded")
        consts = sem("consts")
        xT_ready = sem("xT_ready")
        xT_copied = sem("xT_copied")
        xT_kept = sem("xT_kept")
        first_kept = sem("first_kept")
        A_ready = sem("A_ready")
        A_copied = sem("A_copied")
        xT_back = sem("xT_back")
        B_ready = sem("B_ready")
        B_copied = sem("B_copied")
        A_stored = [sem(f"A_stored{i}") for i in range(NODE_RING)]
        B_stored = [sem(f"B_stored{i}") for i in range(NODE_RING)]
        prep = sem("prep")
        edge_ready = [sem(f"edge_ready{i}") for i in range(3)]
        base_ready = sem("base_ready")
        base_out = sem("base_out")
        base_in = sem("base_in")
        col_ready = sem("col_ready")
        col_copied = sem("col_copied")
        cleared = sem("cleared")
        span_ready = sem("span_ready")
        span_turned = sem("span_turned")
        flag_ready = sem("flag_ready")
        chunks_done = sem("chunks_done")
        idx_staged = sem("idx_staged")
        go = sem("go")
        meta_staged = sem("meta_staged")
        landed = [sem(f"landed{i}") for i in range(ROWS_RING)]
        oh_ready = sem("oh_ready")
        spread_t = sem("spread_t")
        spread_sb = sem("spread_sb")
        win_loaded = [sem(f"win_loaded{i}") for i in range(2)]
        b_split = sem("b_split")
        pre_ready = sem("pre_ready")
        z_ready = sem("z_ready")
        hid_ready = sem("hid_ready")
        sum_ready = sem("sum_ready")
        sum_out = sem("sum_out")
        messages_ready = sem("messages_ready")
        sum_added = sem("sum_added")
        trash_ready = sem("trash_ready")
        table_zero = sem("table_zero")
        abs_ready = sem("abs_ready")
        abs_turned = sem("abs_turned")
        abs_copied = sem("abs_copied")
        table_clear = sem("table_clear")
        tile_step = sem("tile_step")
        tile_landed = sem("tile_landed")
        dst_turned = sem("dst_turned")
        combined = sem("combined")
        old_landed = sem("old_landed")
        scattered = sem("scattered")
        chunk_loaded = sem("chunk_loaded")
        chunk_turned = sem("chunk_turned")
        chunk_staged = sem("chunk_staged")
        chunk_ready = sem("chunk_ready")
        chunk_copied = sem("chunk_copied")
        xe_loaded = [sem(f"xe_loaded{i}") for i in range(NODE_RING)]
        sum_staged = sem("sum_staged")
        back_ready = sem("back_ready")
        y_ready = sem("y_ready")
        st_ready = sem("st_ready")
        mv_ready = sem("mv_ready")
        std_ready = sem("std_ready")
        rstd_ready = sem("rstd_ready")
        shift_ready = sem("shift_ready")
        o_ready = sem("o_ready")
        o_stored = [sem(f"o_stored{i}") for i in range(NODE_RING)]

        block = ctx.enter_context(nc.Block())

        x_main = x[0:(CHUNKS - 1) * P, :].rearrange("(c p) k -> p c k", p=P)
        out_main = out[0:(CHUNKS - 1) * P, :].rearrange("(c p) k -> p c k", p=P)
        A_rows = A_tab.rearrange("(c p) k -> p c k", p=P)
        B_rows = B_tab.rearrange("(c p) k -> p c k", p=P)
        EDGE_LOADS = DMA * (GROUPS + (1 if REST else 0))

        def chunks_in(q):
            return min(4, CHUNKS - 4 * q) if isinstance(q, int) else 4

        def first_chunk(q):
            return 1 if chunks_in(q) > 1 else 0

        def columns(q):
            return bass.ds(q * 4 * P, chunks_in(q) * P)

        def load_nodes(eng, to, q, slot, signal):
            n = chunks_in(q)
            if beyond(q, QUADS - 1):
                if n > 1:
                    eng.dma_start(to[:, slot, 0:n - 1, :], x_main[:, 4 * q:4 * q + n - 1, :]).then_inc(signal, DMA)
                eng.dma_start(to[0:LAST, slot, n - 1, :], x[(CHUNKS - 1) * P:N, :]).then_inc(signal, DMA)
            else:
                eng.dma_start(to[:, slot, :, :], x_main[:, bass.ds(q * 4, 4), :]).then_inc(signal, DMA)

        def transfers(q, slot):
            extra = DMA if beyond(q, QUADS - 1) and chunks_in(q) > 1 else 0
            return rounds(q, slot, NODE_RING, DMA) + DMA + extra

        def all_stored(eng, stored, extra=0):
            for slot in range(NODE_RING):
                uses = len(range(slot, QUADS, NODE_RING))
                eng.wait_ge(stored[slot], DMA * (uses + (extra if slot == (QUADS - 1) % NODE_RING else 0)))

        def load_edges(eng, to, array, g, signal):
            n = min(FULL - g * P, P)
            eng.dma_start(to[0:n, g, :], array[g * P * BLOCK:(g * P + n) * BLOCK]
                          .rearrange("(p b) -> p b", b=BLOCK)).then_inc(signal, DMA)
            if g == g_last and REST:
                r = FULL - g_last * P
                eng.dma_start(to[r:r + 1, g_last, 0:REST],
                              array[FULL * BLOCK:E].rearrange("(p b) -> p b", p=1)).then_inc(signal, DMA)

        def rounds(i, slot, ring, each):
            return (i - slot) * (each // ring)

        def fast_or_general(eng, stretch, nodes, general):
            def fast(cuts):
                firsts = [0] + [cut for cut, _ in cuts]
                first, q = 0, 0
                for cut, quads in cuts + [(BLOCKS, QUADS)]:
                    stretch(first, cut, firsts)
                    nodes(q, quads, sum_added, cut)
                    first, q = cut, quads

            eng.wait_ge(flag_ready, 1)
            span = eng.value_load(span_i[0:1, 0:1], min_val=0, max_val=NP)
            with eng.If(span < WINDOW):
                below = eng.value_load(span_i[0:1, 1:2], min_val=0, max_val=NP)
                with eng.If(below < 1):
                    fast(CUTS)
                with eng.Else():
                    fast([])
            with eng.Else():
                general()
                nodes(0, QUADS, chunks_done, 1)

        @block.sync
        def _(sp):
            sp.dma_start(w1_sb[:, :, :], W1.rearrange("(h k) n -> k h n", h=2)).then_inc(ld_w, DMA)
            sp.dma_start(bias_rows[:, 0, :], b1.rearrange("(a n) -> a n", a=1)).then_inc(ld_w, DMA)
            sp.dma_start(bias_rows[:, 1, :], b2.rearrange("(a n) -> a n", a=1)).then_inc(ld_w, DMA)
            sp.dma_start(w2_sb[:, :], W2).then_inc(ld_w, DMA)
            def load_x(q, slot):
                hold(sp, xT_ready, q - NODE_RING + 1)
                load_nodes(sp, x_in, q, slot, ld_x[slot])

            for q in range(NODE_RING - 1):
                load_x(q, q)

            def x_and_A(q, slot):
                if not beyond(q + NODE_RING - 1, QUADS):
                    load_x(q + NODE_RING - 1, (slot + NODE_RING - 1) % NODE_RING)
                sp.wait_ge(A_copied, q + 1)
                n = chunks_in(q)
                sp.dma_start(A_rows[:, bass.ds(q * 4, n), :], A_sb[:, slot, 0:n, :]).then_inc(A_stored[slot], DMA)
            steps(sp, QUADS, NODE_RING, x_and_A, ahead=NODE_RING)

            sp.wait_ge(base_ready, 1)
            with nc.allow_non_contiguous_dma(reason="512 words, once"):
                sp.dma_start(base_tab.rearrange("(g p) -> p g", p=P), base_i[:, :]).then_inc(base_out, DMA)
            sp.wait_ge(base_out, DMA)
            sp.dma_start(base_row[:, :], base_tab.rearrange("(a n) -> a n", a=1)).then_inc(base_in, DMA)
            sp.wait_ge(base_in, DMA)

            def store_B(q, slot):
                sp.wait_ge(B_copied, q + 1)
                n = chunks_in(q)
                sp.dma_start(B_rows[:, bass.ds(q * 4, n), :], B_sb[:, slot, 0:n, :]).then_inc(B_stored[slot], DMA)
            steps(sp, QUADS, NODE_RING, store_B, ahead=1)
            all_stored(sp, B_stored)

            def load_window(s, slot):
                base = sp.value_load(base_row[0:1, bass.ds(s, 1)], min_val=0, max_val=NP - WINDOW)
                hold(sp, b_split, 4 * (s - 1))
                for h in range(2):
                    sp.dma_start(b_win[h * WINDOW:(h + 1) * WINDOW, slot, :],
                                 B_tab[bass.ds(base, WINDOW), :]).then_inc(win_loaded[slot], DMA)

            def zero_and_read_sums():
                sp.wait_ge(table_zero, 1)
                with sp.Fori(0, CHUNKS + 1) as c:
                    sp.dma_start(sum_tab[bass.ds(c * P, P), :], zero_row).then_inc(table_clear, DMA)
                sp.wait_ge(scattered, DMA * EDGE_COLS)
                with sp.Fori(0, CHUNKS) as c:
                    sp.dma_start(sum_old, sum_tab[bass.ds(c * P, P), :]).then_inc(chunk_loaded, DMA)
                    sp.wait_ge(chunk_copied, c + 1)
                    sp.sem_inc(go, 1)

            def load_windows(first, last, firsts):
                steps(sp, min(last + 2, BLOCKS), 2, load_window, first=first + 2 if first else 0)

            def load_x_again(q, slot):
                hold(sp, y_ready, q - NODE_RING + 1)
                load_nodes(sp, xe, q, slot, xe_loaded[slot])

            def store_out(q, slot):
                sp.wait_ge(o_ready, q + 1)
                n = chunks_in(q)
                if beyond(q, QUADS - 1):
                    if n > 1:
                        sp.dma_start(out_main[:, 4 * q:4 * q + n - 1, :],
                                     y[:, slot, 0:n - 1, :]).then_inc(o_stored[slot], DMA)
                    sp.dma_start(out[(CHUNKS - 1) * P:N, :], y[0:LAST, slot, n - 1, :]).then_inc(o_stored[slot], DMA)
                else:
                    sp.dma_start(out_main[:, bass.ds(q * 4, 4), :], y[:, slot, :, :]).then_inc(o_stored[slot], DMA)

            def nodes(first, last, sums, done):
                if first == 0:
                    sp.wait_ge(sums, 1)
                for q in range(first, min(first + NODE_RING - 1, last)):
                    load_x_again(q, q % NODE_RING)

                def x_and_out(q, slot):
                    if not beyond(q + NODE_RING - 1, last):
                        load_x_again(q + NODE_RING - 1, (slot + NODE_RING - 1) % NODE_RING)
                    store_out(q, slot)
                steps(sp, last, NODE_RING, x_and_out, ahead=NODE_RING, first=first)

            fast_or_general(sp, load_windows, nodes, zero_and_read_sums)
            all_stored(sp, o_stored, extra=1 if chunks_in(QUADS - 1) > 1 else 0)

        @block.gpsimd
        def _(pool):
            nc.gpsimd.memset(ident[:, :], 0.0).then_inc(consts, 1)
            nc.gpsimd.memset(ones[:, :], 1.0).then_inc(consts, 1)
            pool.wait_ge(consts, 2)
            nc.gpsimd.affine_select(out=ident[:, :], in_=ident[:, :], compare_op=ALU.not_equal, fill=1.0,
                                    base=0, pattern=[[-1, P]], channel_multiplier=1).then_inc(consts, 1)
            nc.gpsimd.iota(window_iota[:, :], pattern=[[1, WINDOW]], base=0, channel_multiplier=0,
                           allow_small_or_imprecise_dtypes=True).then_inc(consts, 1)
            nc.gpsimd.iota(block_no[:, :], pattern=[[P, GROUPS]], base=0, channel_multiplier=1,
                           allow_small_or_imprecise_dtypes=True).then_inc(consts, 1)
            pool.wait_ge(consts, 5)
            for h in range(2):
                half = slice(h * WINDOW, (h + 1) * WINDOW)
                nc.gpsimd.tensor_copy(fold[half, :], ident[half, half]).then_inc(consts, 1)

            def keep_xT(q, slot):
                pool.wait_ge(xT_copied, q + 1)
                n, one = chunks_in(q), first_chunk(q)
                nc.gpsimd.tensor_copy(sumT[:, bass.ds((q * 4 + one) * P, (n - one) * P)],
                                      xT_sb[:, slot % 2, one:n, :].rearrange("p c n -> p (c n)")).then_inc(xT_kept, 1)
            steps(pool, QUADS, NODE_RING, keep_xT, ahead=1)
            all_stored(pool, A_stored)

            def gather(s, slot):
                pool.wait_ge(idx_staged, s + 1)
                hold(pool, z_ready, s - ROWS_RING + 1)
                pool.sem_inc(go, 1)
                for t in range(TILES):
                    nc.gpsimd.indirect_dma_start(
                        out=rows[:, slot, t, :], out_offset=None, in_=A_tab,
                        in_offset=bass.IndirectOffsetOnAxis(ap=src_now[:, slot, t:t + 1], axis=0),
                    ).then_inc(landed[slot], DMA)

            def general():
                nc.gpsimd.iota(trash, pattern=[[0, 1]], base=NP, channel_multiplier=1,
                               allow_small_or_imprecise_dtypes=True).then_inc(trash_ready, 1)
                nc.gpsimd.affine_select(out=before, in_=ones[:, :], compare_op=ALU.is_gt, fill=0.0, base=0,
                                        pattern=[[-1, P]], channel_multiplier=1).then_inc(trash_ready, 1)
                pool.wait_ge(table_clear, DMA * (CHUNKS + 1))
                all_stored(pool, B_stored)
                with pool.Fori(0, EDGE_COLS) as t:
                    pool.wait_ge(tile_step, TILE_STEPS * t + 4)
                    pool.sem_inc(go, 1)
                    for to, table, k in ((a_rows, A_tab, 0), (b_rows, B_tab, 1)):
                        nc.gpsimd.indirect_dma_start(
                            out=to, out_offset=None, in_=table,
                            in_offset=bass.IndirectOffsetOnAxis(ap=index_now[:, k:k + 1], axis=0),
                        ).then_inc(tile_landed, DMA)
                    pool.wait_ge(tile_step, TILE_STEPS * t + INDEX_STEP)
                    pool.sem_inc(go, 1)
                    nc.gpsimd.indirect_dma_start(
                        out=sum_old, out_offset=None, in_=sum_tab,
                        in_offset=bass.IndirectOffsetOnAxis(ap=index_now[:, 2:3], axis=0),
                    ).then_inc(old_landed, DMA)
                    pool.wait_ge(tile_step, TILE_STEPS * t + TILE_STEPS)
                    pool.sem_inc(go, 1)
                    nc.gpsimd.indirect_dma_start(
                        out=sum_tab, out_offset=bass.IndirectOffsetOnAxis(ap=index_now[:, 2:3], axis=0),
                        in_=sum_new, in_offset=None).then_inc(scattered, DMA)

            pool.wait_ge(flag_ready, 1)
            span = pool.value_load(span_i[0:1, 0:1], min_val=0, max_val=NP)
            with pool.If(span < WINDOW):
                steps(pool, BLOCKS, ROWS_RING, gather)
            with pool.Else():
                general()

        @block.scalar
        def _(act):
            act.wait_ge(bias_turned, 1)
            nc.scalar.copy(bias_wide[:, :, :], win_ps[:, 0, 0:2 * D].rearrange("p (b n) -> p b n", b=2)
                           ).then_inc(bias_ready, 1)

            def copy_xT(q, slot):
                act.wait_ge(xT_ready, q + 1)
                hold(act, A_ready, q - 1)
                hold(act, xT_kept, q - 1)
                n = chunks_in(q)
                if first_chunk(q):
                    nc.scalar.copy(sumT[:, bass.ds(q * 4 * P, P)], xT_ps[:, slot % 2, 0, :]).then_inc(first_kept, 1)
                nc.scalar.copy(xT_sb[:, slot % 2, 0:n, :], xT_ps[:, slot % 2, 0:n, :]).then_inc(xT_copied, 1)

            copy_xT(0, 0)

            def first_table(q, slot):
                if not beyond(q + 1, QUADS):
                    copy_xT(q + 1, (slot + 1) % NODE_RING)
                act.wait_ge(A_ready, q + 1)
                hold(act, A_stored[slot], rounds(q, slot, NODE_RING, DMA))
                n = chunks_in(q)
                nc.scalar.copy(A_sb[:, slot, 0:n, :], tab_ps[:, slot % 2, 0:n, :]).then_inc(A_copied, 1)
            act.wait_ge(padded, 3)
            for g in range(GROUPS):
                load_edges(act, src_i, src, g, ld_edge[1])
                load_edges(act, dst_i, dst, g, ld_edge[0])
                first_table(g, g % NODE_RING)
            steps(act, QUADS, NODE_RING, first_table, ahead=2, first=GROUPS)
            all_stored(act, A_stored)
            for g in range(GROUPS):
                load_edges(act, w_f, edge_weight, g, ld_edge[2])

            def xT_again(q, slot):
                act.wait_ge(A_ready, QUADS)
                act.wait_ge(xT_kept, QUADS)
                act.wait_ge(first_kept, QUADS - (0 if first_chunk(QUADS - 1) else 1))
                hold(act, B_ready, q - 1)
                n = chunks_in(q)
                nc.scalar.copy(xT_sb[:, slot % 2, 0:n, :], sumT[:, columns(q)]
                               .rearrange("p (c n) -> p c n", c=n)).then_inc(xT_back, 1)
            steps(act, QUADS, NODE_RING, xT_again, ahead=1)

            def copy_spread(s, slot):
                act.wait_ge(spread_t, s + 1)
                hold(act, pre_ready, s - 1)
                hold(act, sum_out, 2 * (s - RING + 1))
                nc.scalar.activation(spread[:, slot % 2, :, :], spread_ps[:, slot % 2, :, :], ACT.Copy,
                                     accum_out=count[:, slot, :]).then_inc(spread_sb, 1)

            def copy_sums(s, slot):
                act.wait_ge(sum_ready, s + 1)
                hold(act, messages_ready, s - 1)
                nc.scalar.copy(win_sum[:, slot % 2, :], win_ps[:, slot % 2, 0:WINDOW]).then_inc(sum_out, 1)
                nc.scalar.activation(fold_count[:, slot % 2, :], fold[:, :], ACT.Copy,
                                     scale=count[:, slot, :]).then_inc(sum_out, 1)

            def hidden(s, slot):
                act.wait_ge(z_ready, s + 1)
                here = hid[:, slot % 2, :, :]
                nc.scalar.activation(here, here, ACT.Relu).then_inc(hid_ready, 1)
                if not beyond(s + 2, BLOCKS):
                    copy_spread(s + 2, (slot + 2) % RING)

            def edges(first, last, firsts):
                if first == 0:
                    copy_spread(0, 0)
                    copy_spread(1, 1)

                def sums_and_hidden(s, slot):
                    if not opens(s, firsts):
                        copy_sums(s - 1, (slot - 1) % RING)
                    hidden(s, slot)
                steps(act, last, RING, sums_and_hidden, ahead=2 if last == BLOCKS else 0, first=first)
                copy_sums(last - 1, (last - 1) % RING)

            def stage_sum(q, slot):
                hold(act, back_ready, q - 1)
                n = chunks_in(q)
                nc.scalar.copy(sum_now[:, slot % 2, 0:n, :], sumT[:, columns(q)]
                               .rearrange("p (c n) -> p c n", c=n)).then_inc(sum_staged, 1)

            def stdev(q, slot):
                act.wait_ge(mv_ready, q + 1)
                hold(act, rstd_ready, q - 1)
                n = chunks_in(q)
                nc.scalar.activation(std[:, slot % 2, 0:n], mv[:, slot % 2, 0:n, 1], ACT.Sqrt,
                                     bias=eps_col[:, 0:1], scale=1.0).then_inc(std_ready, 1)

            def scale(q, slot):
                act.wait_ge(shift_ready, q + 1)
                for c in range(chunks_in(q)):
                    last = nc.scalar.activation(y[:, slot, c, :], y[:, slot, c, :], ACT.Identity,
                                                scale=rstd[:, slot % 2, c:c + 1], bias=shift[:, slot % 2, c:c + 1])
                last.then_inc(o_ready, 1)

            def nodes(first, last, sums, done):
                act.wait_ge(sums, done)
                stage_sum(first, first % NODE_RING)

                def stage_and_scale(q, slot):
                    if not beyond(q + 1, last):
                        stage_sum(q + 1, (slot + 1) % NODE_RING)
                    stdev(q, slot)
                    if not opens(q, [first]):
                        scale(q - 1, (slot - 1) % NODE_RING)
                steps(act, last, NODE_RING, stage_and_scale, ahead=2, first=first)
                scale(last - 1, (last - 1) % NODE_RING)

            fast_or_general(act, edges, nodes, lambda: None)

        @block.vector
        def _(dve):
            nc.vector.memset(dst_i[:, g_last, :], -1).then_inc(padded, 1)
            nc.vector.memset(src_f[:, g_last, :], 0.0).then_inc(padded, 1)
            nc.vector.memset(w_f[:, g_last, :], 0.0).then_inc(padded, 1)
            nc.vector.memset(zeros[:, :], 0.0).then_inc(padded, 1)
            nc.vector.memset(eps_col[:, :], EPS).then_inc(padded, 1)

            done = [0]

            def step(instruction):
                done[0] += 1
                instruction.then_inc(prep, 1)
                dve.wait_ge(prep, done[0])

            dve.wait_ge(ld_edge[1], EDGE_LOADS)
            for g in range(GROUPS):
                nc.vector.tensor_copy(src_f[:, g, :], src_i[:, g, :]).then_inc(edge_ready[1], 1)
            dve.wait_ge(ld_edge[0], EDGE_LOADS)
            for g in range(GROUPS):
                step(nc.vector.tensor_copy(dst_f[:, g, :], dst_i[:, g, :]))
                if g == g_last:
                    step(nc.vector.tensor_scalar(min_tmp, dst_f[:, g, :], 0.0, float(2 * NP),
                                                 ALU.is_lt, ALU.mult))
                    step(nc.vector.tensor_tensor(min_tmp, min_tmp, dst_f[:, g, :], ALU.add))
                    step(nc.vector.tensor_reduce(lo[:, g:g + 1], min_tmp, AX.X, ALU.min))
                else:
                    step(nc.vector.tensor_reduce(lo[:, g:g + 1], dst_f[:, g, :], AX.X, ALU.min))
                step(nc.vector.tensor_reduce(hi[:, g:g + 1], dst_f[:, g, :], AX.X, ALU.max))
            dve.wait_ge(consts, 5)
            nc.vector.memset(lowest_by[:, 0, :], 0.0).then_inc(prep, 1)
            done[0] += 1
            for k, (cut, quads) in enumerate(CUTS):
                nodes_more = (quads - (CUTS[k - 1][1] if k else 0)) * 4 * P
                step(nc.vector.tensor_scalar(lowest[:, :], block_no[:, :], float(cut), float(nodes_more),
                                             ALU.is_ge, ALU.mult))
                step(nc.vector.tensor_tensor(lowest_by[:, k + 1, :], lowest_by[:, k, :], lowest[:, :], ALU.add))
            step(nc.vector.tensor_scalar(base_f[:, :], lo[:, :], float(NP - WINDOW), None, ALU.min))
            nc.vector.tensor_copy(base_i[:, :], base_f[:, :]).then_inc(base_ready, 1)
            step(nc.vector.tensor_tensor(span[:, :], hi[:, :], base_f[:, :], ALU.subtract))
            nc.vector.tensor_reduce(span_p[:, 0:1], span[:, :], AX.X, ALU.max).then_inc(span_ready, 1)
            step(nc.vector.tensor_tensor(lowest[:, :], lowest_by[:, len(CUTS), :], base_f[:, :], ALU.subtract))
            nc.vector.tensor_reduce(span_p[:, 1:2], lowest[:, :], AX.X, ALU.max).then_inc(span_ready, 1)
            for g in range(GROUPS):
                nc.vector.tensor_scalar(dst_f[:, g, :], dst_f[:, g, :], base_f[:, g:g + 1], None,
                                        ALU.subtract).then_inc(edge_ready[0], 1)

            dve.wait_ge(span_turned, 1)
            step(nc.vector.tensor_reduce(span_one[:, :], win_ps[0:1, 0, 0:2 * P]
                                         .rearrange("a (k p) -> a k p", k=2), AX.X, ALU.max))
            step(nc.vector.tensor_scalar(span_one[:, :], span_one[:, :], 0.0, None, ALU.max))
            nc.vector.tensor_copy(span_i[:, :], span_one[:, :]).then_inc(flag_ready, 1)

            def copy_columns(some):
                for j in some:
                    a, g, h = COLS[j]
                    n = min(BLOCKS - g * P, P)
                    dve.wait_ge(col_ready, j + 1)
                    to = src_col if a == 1 else meta[:, :, 0 if a == 0 else 1, :]
                    nc.vector.tensor_copy(to[:, g * P:g * P + n, h * HALF:(h + 1) * HALF],
                                          col_ps[:, j % 2, :, 0:n].rearrange("p t b -> p b t")).then_inc(col_copied, 1)

            copy_columns(SRC_COLS)

            def stage_index(s, slot):
                nc.vector.tensor_copy(src_now[:, slot, :], src_col[:, bass.ds(s, 1), :]
                                      .rearrange("p a t -> p (a t)")).then_inc(idx_staged, 1)

            def stage_meta(s, slot):
                hold(dve, z_ready, s - RING + 1)
                nc.vector.tensor_copy(meta_now[:, slot, :, :], meta[:, bass.ds(s, 1), :, :]
                                      .rearrange("p a m t -> p (a m) t")).then_inc(meta_staged, 1)

            def one_hots(s, slot):
                dve.wait_ge(meta_staged, s + 1)
                hold(dve, sum_ready, s - RING + 1)
                for t in range(TILES):
                    last = nc.vector.tensor_scalar(onehot[:, slot, t % HALF, t // HALF, :], window_iota[:, :],
                                                   meta_now[:, slot, 0, t:t + 1], None, ALU.is_equal)
                last.then_inc(oh_ready, 1)

            def pre_hidden(s, slot):
                dve.wait_ge(pre_ready, s + 1)
                dve.wait_ge(landed[slot], rounds(s, slot, ROWS_RING, DMA * TILES) + DMA * TILES)
                hold(dve, sum_ready, s - 1)
                for t in range(TILES):
                    last = nc.vector.scalar_tensor_tensor(
                        out=hid[:, slot % 2, t, :], in0=rows[:, slot, t, :], scalar=meta_now[:, slot % RING, 1, t:t + 1],
                        in1=pre_ps[:, slot % 2, t, :], op0=ALU.mult, op1=ALU.add)
                last.then_inc(z_ready, 1)

            def add_sums(s, slot):
                base = dve.value_load(base_row[0:1, bass.ds(s, 1)], min_val=0, max_val=NP - WINDOW)
                dve.wait_ge(messages_ready, s + 1)
                hold(dve, sum_added, s)
                to = sumT[:, bass.ds(base, WINDOW)]
                nc.vector.tensor_tensor(to, to, win_ps[:, slot, WINDOW:2 * WINDOW], ALU.add).then_inc(sum_added, 1)

            def split_window(s, slot, part):
                if part == 0:
                    dve.wait_ge(win_loaded[slot], rounds(s, slot, 2, 2 * DMA) + 2 * DMA)
                    hold(dve, pre_ready, s - 1)
                else:
                    dve.wait_ge(b_split, 4 * s + part)
                if part % 2 == 0:
                    left = b_win if part == 0 else b_left
                    nc.vector.tensor_copy(b_part[:, slot, part // 2, :], left[:, slot, :]).then_inc(b_split, 1)
                else:
                    left, to = (b_win[:, slot, :], b_left[:, slot, :]) if part == 1 else \
                        (b_left[:, slot, :], b_part[:, slot, 2, :])
                    nc.vector.tensor_tensor(to, left, b_part[:, slot, part // 2, :],
                                            ALU.subtract).then_inc(b_split, 1)

            def edges(s, slot, firsts):
                if not beyond(s + ROWS_RING - 1, BLOCKS):
                    stage_index(s + ROWS_RING - 1, (slot + ROWS_RING - 1) % ROWS_RING)
                ahead = not beyond(s + 2, BLOCKS)
                if ahead:
                    stage_meta(s + 2, (slot + 2) % RING)
                    split_window(s + 2, slot % 2, 0)
                    one_hots(s + 2, (slot + 2) % RING)
                    split_window(s + 2, slot % 2, 1)
                pre_hidden(s, slot)
                if ahead:
                    split_window(s + 2, slot % 2, 2)
                if not opens(s, firsts):
                    add_sums(s - 1, (slot - 1) % 2)
                if ahead:
                    split_window(s + 2, slot % 2, 3)

            def second_table(q, slot, clear=False):
                dve.wait_ge(xT_back, q + 1)
                dve.wait_ge(B_ready, q + 1)
                hold(dve, B_stored[slot], rounds(q, slot, NODE_RING, DMA))
                for c in range(chunks_in(q)):
                    last = nc.vector.tensor_tensor(B_sb[:, slot, c, :], bias_wide[:, 0, :], tab_ps[:, slot % 2, c, :],
                                                   ALU.add)
                last.then_inc(B_copied, 1)
                if clear:
                    nc.vector.tensor_copy(sumT[:, columns(q)], zeros[:, 0:chunks_in(q) * P]).then_inc(cleared, 1)

            def before_edges():
                dve.wait_ge(col_copied, len(SRC_COLS))
                for s in range(ROWS_RING - 1):
                    stage_index(s, s)
                copy_columns(OTHER_COLS)
                dve.wait_ge(col_copied, len(COLS))
                for s in range(2):
                    stage_meta(s, s)
                    one_hots(s, s)
                dve.wait_ge(bias_ready, 1)
                steps(dve, QUADS, NODE_RING, lambda q, slot: second_table(q, slot, clear=True), ahead=1)
                dve.wait_ge(cleared, QUADS)
                all_stored(dve, B_stored)
                dve.wait_ge(base_in, DMA)
                for s in range(2):
                    for part in range(4):
                        split_window(s, s, part)

            def all_edges(first, last, firsts):
                if first == 0:
                    before_edges()
                steps(dve, last, ROWS_RING, lambda s, slot: edges(s, slot, firsts),
                      ahead=ROWS_RING - 1 if last == BLOCKS else 0, first=first)
                add_sums(last - 1, (last - 1) % 2)

            def general():
                copy_columns(OTHER_COLS)
                dve.wait_ge(col_copied, len(COLS))
                dve.wait_ge(bias_ready, 1)
                steps(dve, QUADS, NODE_RING, second_table, ahead=1)
                dve.wait_ge(xT_kept, QUADS)
                all_stored(dve, A_stored)
                nc.vector.memset(zero_row, 0.0).then_inc(table_zero, 1)
                nc.vector.memset(hid_one[:, D:D + 1], 1.0).then_inc(abs_copied, 1)
                for g in range(GROUPS):
                    nc.vector.tensor_scalar(dst_f[:, g, :], dst_f[:, g, :], base_f[:, g:g + 1], None,
                                            ALU.add).then_inc(abs_ready, 1)
                nc.vector.tensor_copy(w_cols.rearrange("p (b t) -> p b t", t=TILES),
                                      meta[:, :, 1, :]).then_inc(abs_copied, 1)
                for j in range(2 * GROUPS):
                    g, h = j // 2, j % 2
                    n = min(BLOCKS - g * P, P)
                    dve.wait_ge(abs_turned, j + 1)
                    nc.vector.tensor_copy(dst_cols.rearrange("p (b t) -> p b t", t=TILES)
                                          [:, g * P:g * P + n, h * HALF:(h + 1) * HALF],
                                          col_ps[:, j % 2, :, 0:n].rearrange("p t b -> p b t")).then_inc(abs_copied, 1)
                dve.wait_ge(abs_copied, 2 * GROUPS + 2)
                dve.wait_ge(trash_ready, 2)

                with dve.Fori(0, EDGE_COLS) as t:
                    taken = [0]

                    def then(instruction):
                        taken[0] += 1
                        instruction.then_inc(tile_step, 1)
                        dve.wait_ge(tile_step, TILE_STEPS * t + taken[0])

                    then(nc.vector.tensor_copy(dst_now, dst_cols[:, bass.ds(t, 1)]))
                    then(nc.vector.tensor_copy(w_now, w_cols[:, bass.ds(t, 1)]))
                    then(nc.vector.tensor_copy(index_now[:, 0:1], src_cols[:, bass.ds(t, 1)]))
                    then(nc.vector.tensor_scalar(index_now[:, 1:2], dst_now, 0.0, None, ALU.max))
                    then(nc.vector.tensor_scalar(dst_wide, ones[:, :], dst_now, None, ALU.mult))
                    dve.wait_ge(dst_turned, t + 1)
                    then(nc.vector.tensor_scalar(equal, spread_ps[:, 0, 0, :], dst_now, None, ALU.is_equal))
                    then(nc.vector.tensor_tensor(earlier, equal, before, ALU.mult))
                    then(nc.vector.tensor_reduce(n_before, earlier, AX.X, ALU.add))
                    then(nc.vector.tensor_scalar(first, n_before, 0.5, None, ALU.is_lt))
                    then(nc.vector.tensor_scalar(is_edge, dst_now, 0.0, None, ALU.is_ge))
                    then(nc.vector.tensor_tensor(first, first, is_edge, ALU.mult))
                    then(nc.vector.tensor_tensor(at_now, dst_now, trash, ALU.subtract))
                    then(nc.vector.tensor_tensor(at_now, at_now, first, ALU.mult))
                    then(nc.vector.tensor_tensor(index_now[:, 2:3], at_now, trash, ALU.add))
                    assert taken[0] == INDEX_STEP
                    dve.wait_ge(tile_landed, 2 * DMA * t + 2 * DMA)
                    then(nc.vector.scalar_tensor_tensor(out=hid_one[:, 0:D], in0=a_rows, scalar=w_now, in1=b_rows,
                                                        op0=ALU.mult, op1=ALU.add))
                    then(nc.vector.tensor_scalar(hid_one[:, 0:D], hid_one[:, 0:D], 0.0, None, ALU.max))
                    assert taken[0] == INDEX_STEP + 2
                    dve.wait_ge(combined, t + 1)
                    dve.wait_ge(old_landed, DMA * t + DMA)
                    then(nc.vector.tensor_tensor(sum_new, sum_old, win_ps[:, 0, 0:D + 1], ALU.add))
                    assert taken[0] == TILE_STEPS
                    dve.wait_ge(scattered, DMA * t + DMA)

                with dve.Fori(0, CHUNKS) as c:
                    dve.wait_ge(chunk_turned, c + 1)
                    nc.vector.tensor_copy(hid_T, spread_ps[:, 0, 0, :]).then_inc(chunk_staged, 1)
                    nc.vector.tensor_copy(degree_T, spread_ps[0:1, 0, 1, :]).then_inc(chunk_staged, 1)
                    dve.wait_ge(chunk_ready, c + 1)
                    nc.vector.tensor_copy(sumT[:, bass.ds(c * P, P)], win_ps[:, 0, 0:P]).then_inc(chunk_copied, 1)
                dve.wait_ge(chunk_copied, CHUNKS)
                dve.sem_inc(chunks_done, 1)

            def add_x(q, slot):
                dve.wait_ge(back_ready, q + 1)
                dve.wait_ge(xe_loaded[slot], transfers(q, slot))
                hold(dve, o_stored[slot], rounds(q, slot, NODE_RING, DMA))
                n = chunks_in(q)
                nc.vector.tensor_tensor(y[:, slot, 0:n, :], xe[:, slot, 0:n, :],
                                        win_ps[:, slot % 2, 0:n * D].rearrange("p (c d) -> p c d", c=n),
                                        ALU.add).then_inc(y_ready, 1)

            def rstd_and_shift(q, slot):
                dve.wait_ge(std_ready, q + 1)
                hold(dve, o_ready, q - 1)
                n = chunks_in(q)
                nc.vector.reciprocal(rstd[:, slot, 0:n], std[:, slot, 0:n]).then_inc(rstd_ready, 1)
                dve.wait_ge(rstd_ready, q + 1)
                nc.vector.scalar_tensor_tensor(out=shift[:, slot, 0:n], in0=mv[:, slot, 0:n, 0], scalar=-1.0,
                                               in1=rstd[:, slot, 0:n], op0=ALU.mult, op1=ALU.mult
                                               ).then_inc(shift_ready, 1)

            def norm(q, slot, first):
                n = chunks_in(q)
                add_x(q, slot)
                dve.wait_ge(y_ready, q + 1)
                for c in range(n):
                    last = nc.vector.bn_stats(stats[:, slot % 2, c, :], y[:, slot, c, :])
                last.then_inc(st_ready, 1)
                if not opens(q, [first]):
                    rstd_and_shift(q - 1, (slot - 1) % 2)
                dve.wait_ge(st_ready, q + 1)
                dve.sem_inc(go, 1)
                for c in range(n):
                    last = nc.vector.bn_aggr(mv[:, slot % 2, c, :], stats[:, slot % 2, c, :])
                last.then_inc(mv_ready, 1)

            def nodes(first, last, sums, done):
                steps(dve, last, NODE_RING, lambda q, slot: norm(q, slot, first), ahead=1, first=first)
                rstd_and_shift(last - 1, (last - 1) % 2)

            fast_or_general(dve, all_edges, nodes, general)

        @block.tensor
        def _(pe):
            pe.wait_ge(consts, 7)
            pe.wait_ge(ld_w, 4 * DMA)

            nc.tensor.matmul(win_ps[:, 0, 0:2 * D], ones[0:1, :], bias_rows[:, :, :].rearrange("p b n -> p (b n)"),
                             start=True, stop=True).then_inc(bias_turned, 1)

            def transpose_x(q, slot):
                pe.wait_ge(ld_x[slot], transfers(q, slot))
                hold(pe, xT_copied, q - 1)
                for c in range(chunks_in(q)):
                    last = nc.tensor.transpose(xT_ps[:, slot % 2, c, :], x_in[:, slot, c, :], ident[:, :])
                last.then_inc(xT_ready, 1)

            def product(q, slot, half, xT_there, copied, ready):
                pe.wait_ge(xT_there, q + 1)
                hold(pe, copied, q - 1)
                for c in range(chunks_in(q)):
                    last = nc.tensor.matmul(tab_ps[:, slot % 2, c, :], xT_sb[:, slot % 2, c, :], w1_sb[:, half, :],
                                            start=True, stop=True)
                last.then_inc(ready, 1)

            def first_table(q, slot):
                if not beyond(q + 1, QUADS):
                    transpose_x(q + 1, (slot + 1) % NODE_RING)
                product(q, slot, 0, xT_copied, A_copied, A_ready)

            def turn_columns(some):
                for j in some:
                    a, g, h = COLS[j]
                    n = min(BLOCKS - g * P, P)
                    pe.wait_ge(edge_ready[a] if a < 2 else ld_edge[2], g + 1 if a < 2 else EDGE_LOADS)
                    hold(pe, col_copied, j - 1)
                    for t in range(HALF):
                        at = (h * HALF + t) * P
                        last = nc.tensor.transpose(col_ps[:, j % 2, t, 0:n], arrays[0:n, a, g, at:at + P],
                                                   ident[0:n, 0:n])
                    last.then_inc(col_ready, 1)

            transpose_x(0, 0)
            steps(pe, SPLIT, NODE_RING, first_table)
            pe.wait_ge(bias_ready, 1)
            pe.wait_ge(span_ready, 2)
            nc.tensor.transpose(win_ps[0:1, 0, 0:P], span_p[:, 0:1], ident[:, :])
            nc.tensor.transpose(win_ps[0:1, 0, P:2 * P], span_p[:, 1:2], ident[:, :]).then_inc(span_turned, 1)
            for q in range(GROUPS):
                first_table(SPLIT + q, (SPLIT + q) % NODE_RING)
                if q == 0:
                    pe.wait_ge(flag_ready, 1)
                turn_columns(SRC_COLS[2 * q:2 * q + 2])
            steps(pe, QUADS, NODE_RING, first_table, ahead=2, first=SPLIT + GROUPS)
            turn_columns(OTHER_COLS)
            pe.wait_ge(A_copied, QUADS)
            steps(pe, QUADS, NODE_RING, lambda q, slot: product(q, slot, 1, xT_back, B_copied, B_ready))

            def spread_one_hots(s, slot):
                pe.wait_ge(oh_ready, s + 1)
                hold(pe, spread_sb, s - 1)
                for t in range(HALF):
                    last = nc.tensor.transpose(spread_ps[:, slot % 2, t, :], onehot[:, slot, t, :, :]
                                               .rearrange("p h w -> p (h w)"), ident[:, :])
                last.then_inc(spread_t, 1)

            def spread_window(s, slot):
                pe.wait_ge(spread_sb, s + 1)
                pe.wait_ge(b_split, 4 * s + 4)
                hold(pe, z_ready, s - 1)
                for t in range(TILES):
                    h = t // HALF
                    half = slice(h * WINDOW, (h + 1) * WINDOW)
                    for part in range(3):
                        last = nc.tensor.matmul(pre_ps[:, slot, t, :], spread[half, slot, t % HALF, :],
                                                b_part[half, slot, part, :], start=(part == 0), stop=(part == 2))
                last.then_inc(pre_ready, 1)

            def sum_edges(s, slot):
                pe.wait_ge(hid_ready, s + 1)
                hold(pe, sum_out, 2 * (s - 1))
                ring_slot, slot = slot, slot % 2
                for t in range(TILES):
                    last = nc.tensor.matmul(win_ps[:, slot, 0:WINDOW], hid[:, slot, t, :],
                                            onehot[:, ring_slot, t % HALF, t // HALF, :],
                                            start=(t == 0), stop=(t == TILES - 1))
                last.then_inc(sum_ready, 1)

            def messages(s, slot):
                pe.wait_ge(sum_out, 2 * s + 2)
                hold(pe, sum_added, s - 1)
                to = win_ps[:, slot, WINDOW:2 * WINDOW]
                nc.tensor.matmul(to, w2_sb[:, :], win_sum[:, slot, :], start=True, stop=False)
                nc.tensor.matmul(to, bias_wide[:, 1, :], fold_count[:, slot, :], start=False,
                                 stop=True).then_inc(messages_ready, 1)

            def edges(s, slot, firsts):
                if not beyond(s + 2, BLOCKS):
                    spread_one_hots(s + 2, (slot + 2) % RING)
                if not beyond(s + 1, BLOCKS):
                    spread_window(s + 1, (slot + 1) % 2)
                if not opens(s, firsts):
                    messages(s - 1, (slot - 1) % 2)
                sum_edges(s, slot)

            def all_edges(first, last, firsts):
                if first == 0:
                    spread_one_hots(0, 0)
                    spread_one_hots(1, 1)
                    spread_window(0, 0)
                steps(pe, last, RING, lambda s, slot: edges(s, slot, firsts),
                      ahead=2 if last == BLOCKS else 0, first=first)
                messages(last - 1, (last - 1) % 2)

            def general():
                for j in range(2 * GROUPS):
                    g, h = j // 2, j % 2
                    n = min(BLOCKS - g * P, P)
                    pe.wait_ge(abs_ready, g + 1)
                    hold(pe, abs_copied, j + 1)
                    for t in range(HALF):
                        at = (h * HALF + t) * P
                        last = nc.tensor.transpose(col_ps[:, j % 2, t, 0:n], dst_f[0:n, g, at:at + P],
                                                   ident[0:n, 0:n])
                    last.then_inc(abs_turned, 1)
                with pe.Fori(0, EDGE_COLS) as t:
                    pe.wait_ge(tile_step, TILE_STEPS * t + 5)
                    nc.tensor.transpose(spread_ps[:, 0, 0, :], dst_wide, ident[:, :]).then_inc(dst_turned, 1)
                    pe.wait_ge(tile_step, TILE_STEPS * t + INDEX_STEP + 2)
                    nc.tensor.matmul(win_ps[:, 0, 0:D + 1], equal, hid_one, start=True,
                                     stop=True).then_inc(combined, 1)
                with pe.Fori(0, CHUNKS) as c:
                    pe.wait_ge(chunk_loaded, DMA * c + DMA)
                    nc.tensor.transpose(spread_ps[:, 0, 0, :], sum_old[:, 0:D], ident[:, :])
                    nc.tensor.transpose(spread_ps[0:1, 0, 1, :], sum_old[:, D:D + 1],
                                        ident[:, :]).then_inc(chunk_turned, 1)
                    pe.wait_ge(chunk_staged, 2 * c + 2)
                    nc.tensor.matmul(win_ps[:, 0, 0:P], w2_sb[:, :], hid_T, start=True, stop=False)
                    nc.tensor.matmul(win_ps[:, 0, 0:P], bias_rows[:, 1, :], degree_T, start=False,
                                     stop=True).then_inc(chunk_ready, 1)

            def turn_back(q, slot):
                pe.wait_ge(sum_staged, q + 1)
                hold(pe, y_ready, q - 1)
                for c in range(chunks_in(q)):
                    last = nc.tensor.transpose(win_ps[:, slot % 2, c * D:(c + 1) * D], sum_now[:, slot % 2, c, :],
                                               ident[:, :])
                last.then_inc(back_ready, 1)

            def nodes(first, last, sums, done):
                steps(pe, last, NODE_RING, turn_back, ahead=1, first=first)
                pe.wait_ge(y_ready, last)

            fast_or_general(pe, all_edges, nodes, general)


_INS = ['x', 'src', 'dst', 'edge_weight', 'L0_gnn_W1', 'L0_gnn_b1', 'L0_gnn_W2', 'L0_gnn_b2']


def kernel(**inputs):
    import numpy as _np
    import concourse.bacc as _bacc
    from concourse import mybir as _mybir
    from concourse.bass_utils import run_bass_kernel_spmd as _run

    nc = _bacc.Bacc("TRN2", target_bir_lowering=False, num_devices=1)
    arrays, args = {}, []
    for name in _INS:
        a = _np.ascontiguousarray(inputs[name])
        arrays[f"in_{name}_dram"] = a
        args.append(nc.dram_tensor(f"in_{name}_dram", a.shape, _mybir.dt.from_np(a.dtype), kind="ExternalInput").ap())
    args.append(nc.dram_tensor("out_0_dram", arrays["in_x_dram"].shape, F32, kind="ExternalOutput").ap())
    gnn_kernel(nc, *args)
    r = _run(nc, [arrays], core_ids=[0])
    return r.results[0]["out_0_dram"]
```
